# Optimizing a Trainium2 kernel written in Bass

```python
import numpy as np
import jax
import jax.numpy as jnp

def _softmax(x, axis=-1):
    return jax.nn.softmax(x, axis=axis)

def _gelu(x):
    return jax.nn.gelu(x, approximate=True)

def _silu(x):
    return jax.nn.silu(x)

def _sigmoid(x):
    return jax.nn.sigmoid(x)

def _layernorm(x, axis=-1, eps=1e-05):
    m = jnp.mean(x, axis=axis, keepdims=True)
    v = jnp.var(x, axis=axis, keepdims=True)
    return (x - m) / jnp.sqrt(v + eps)

def _scatter_add(tgt, idx, src, axis=0):
    return tgt.at[idx].add(src)

def _segment_sum(src, seg, n):
    return jax.ops.segment_sum(src, seg, n)
kernel_name = 'mk_flamingo_gated_d1_seqx_r4_bf30a1'

def setup_inputs(seed: int=0):
    np.random.seed(seed)
    _w = jnp.asarray

    def _rec_inputs():
        import jax
        import jax.numpy as jnp
        _rk = jax.random.key(seed)
        x = -0.0003929 + 0.9999 * jax.random.normal(jax.random.fold_in(_rk, 1), (16, 128, 256), jnp.float32)
        _lenS = 128 - jax.random.randint(jax.random.fold_in(_rk, 7), (16,), 0, max(1, 128 // 4) + 1, jnp.int32)
        _lenS2 = 128 - jax.random.randint(jax.random.fold_in(_rk, 8), (16,), 0, max(1, 128 // 4) + 1, jnp.int32)
        _ctx_1024P = jax.random.normal(jax.random.fold_in(_rk, 11), (16, 16, 256), jnp.float32)
        _ctx_1024c = jax.random.dirichlet(jax.random.fold_in(_rk, 511), 0.3 * jnp.ones((16,), jnp.float32), (16, 128))
        _ctx_1024t = jnp.einsum('bsk,bkd->bsd', _ctx_1024c, _ctx_1024P)
        _ctx_1024t = _ctx_1024t * jax.lax.rsqrt(jnp.mean(jnp.square(_ctx_1024t)) + 1e-12) * 0.953939
        ctx_1024 = 2.81802e-05 + 1.00001 * (_ctx_1024t + 0.3 * jax.random.normal(jax.random.fold_in(_rk, 611), (16, 128, 256), jnp.float32))
        _g = jax.random.normal(jax.random.fold_in(_rk, 9001), (2, 1), jnp.float32)
        _g = jnp.sign(_g) * jnp.maximum(jnp.abs(_g), 1.0) + (_g == 0) * 1.0
        g_xattn = _g[0]
        g_ffn = _g[1]
        return (x, ctx_1024, g_xattn, g_ffn)
    x, ctx_1024, g_xattn, g_ffn = _rec_inputs()

    def _L0_xattn_setup():
        import jax, jax.numpy as jnp
        import numpy as np
        WINDOW_SIZE = 20
        NEG_BIG = -100000000.0

        def band_mask(S):
            idx = jnp.arange(S)
            return jnp.where(jnp.abs(idx[:, None] - idx[None, :]) <= WINDOW_SIZE, 0.0, NEG_BIG).astype(jnp.float32)
        key = jax.random.key(seed)
        k1, k2, k3, k4 = jax.random.split(key, 4)
        B, S, Dq, Dk = (8, 512, 256, 256)
        queries = jax.random.normal(k1, (B, S, Dq), dtype=jnp.float32)
        keys = jax.random.normal(k2, (B, S, Dk), dtype=jnp.float32)
        lim = 1.0 / np.sqrt(Dk)
        W_reduce = jax.random.uniform(k3, (Dq, Dk), jnp.float32, -lim, lim)
        b_reduce = jax.random.uniform(k4, (Dq,), jnp.float32, -lim, lim)
        return {'queries': queries, 'keys': keys, 'W_reduce': W_reduce, 'b_reduce': b_reduce}
    _L0_xattn_all = _L0_xattn_setup()
    _L0_xattn_in = {k: v for k, v in _L0_xattn_all.items() if k in ('W_reduce', 'b_reduce')}
    del _L0_xattn_all

    def _L0_ffn_setup():
        import jax, jax.numpy as jnp
        import numpy as np
        FEATURES = 256
        D_IN = 256

        def fp8_gemm_optimized(x, input_scale, kernel, kernel_scale):
            s_in = input_scale[0]
            s_k = kernel_scale[0]
            x_q = (x.astype(jnp.float32) / s_in).astype(jnp.float8_e4m3fn)
            k_q = (kernel.astype(jnp.float32) / s_k).astype(jnp.float8_e4m3fn)
            y = jnp.dot(x_q.astype(jnp.float32), k_q.astype(jnp.float32), preferred_element_type=jnp.float32)
            return y * (s_in * s_k)
        key = jax.random.key(seed)
        kx, kk, kb = jax.random.split(key, 3)
        x = jax.random.normal(kx, (4, 2048, D_IN), dtype=jnp.float32)
        limit = np.sqrt(6.0 / (D_IN + FEATURES)).astype(np.float32)
        kernel = jax.random.uniform(kk, (D_IN, FEATURES), dtype=jnp.float32, minval=-limit, maxval=limit).astype(jnp.bfloat16)
        input_scale = jnp.ones((1,), dtype=jnp.float32)
        kernel_scale = jnp.ones((1,), dtype=jnp.float32)
        bias = jnp.zeros((FEATURES,), dtype=jnp.bfloat16)
        return {'x': x, 'kernel': kernel, 'input_scale': input_scale, 'kernel_scale': kernel_scale, 'bias': bias}
    _L0_ffn_all = _L0_ffn_setup()
    _L0_ffn_in = {k: v for k, v in _L0_ffn_all.items() if k in ('kernel', 'input_scale', 'kernel_scale', 'bias')}
    del _L0_ffn_all
    return {'x': x, 'ctx_1024': ctx_1024, 'g_xattn': g_xattn, 'g_ffn': g_ffn, 'L0_xattn_W_reduce': _L0_xattn_in['W_reduce'], 'L0_xattn_b_reduce': _L0_xattn_in['b_reduce'], 'L0_ffn_kernel': _L0_ffn_in['kernel'], 'L0_ffn_input_scale': _L0_ffn_in['input_scale'], 'L0_ffn_kernel_scale': _L0_ffn_in['kernel_scale'], 'L0_ffn_bias': _L0_ffn_in['bias']}

def reference(x, ctx_1024, g_xattn, g_ffn, L0_xattn_W_reduce, L0_xattn_b_reduce, L0_ffn_kernel, L0_ffn_input_scale, L0_ffn_kernel_scale, L0_ffn_bias):
    import jax
    import jax.numpy as jnp

    def _L0_xattn_ref(queries, keys, W_reduce, b_reduce):
        import jax, jax.numpy as jnp
        import numpy as np
        WINDOW_SIZE = 20
        NEG_BIG = -100000000.0

        def band_mask(S):
            idx = jnp.arange(S)
            return jnp.where(jnp.abs(idx[:, None] - idx[None, :]) <= WINDOW_SIZE, 0.0, NEG_BIG).astype(jnp.float32)
        values = keys
        keys_r = jnp.einsum('bkd,qd->bkq', keys, W_reduce) + b_reduce
        sims = jnp.einsum('bqd,bkd->bqk', queries, keys_r)
        sims = sims + band_mask(queries.shape[1])
        weights = jax.nn.softmax(sims, axis=-1)
        return jnp.einsum('bqk,bkd->bqd', weights, values)

    def _L0_ffn_ref(x, kernel, input_scale, kernel_scale, bias):
        import jax, jax.numpy as jnp
        import numpy as np
        FEATURES = 256
        D_IN = 256

        def fp8_gemm_optimized(x, input_scale, kernel, kernel_scale):
            s_in = input_scale[0]
            s_k = kernel_scale[0]
            x_q = (x.astype(jnp.float32) / s_in).astype(jnp.float8_e4m3fn)
            k_q = (kernel.astype(jnp.float32) / s_k).astype(jnp.float8_e4m3fn)
            y = jnp.dot(x_q.astype(jnp.float32), k_q.astype(jnp.float32), preferred_element_type=jnp.float32)
            return y * (s_in * s_k)
        dtype = jnp.bfloat16
        x = x.astype(dtype)
        orig_shape = x.shape
        x2 = x.reshape(-1, x.shape[-1])
        y = fp8_gemm_optimized(x2, input_scale, kernel, kernel_scale)
        y = y.astype(dtype) + bias
        return y.reshape(orig_shape[:-1] + (FEATURES,))
    x = x + jnp.tanh(g_xattn[0]) * _L0_xattn_ref(_layernorm(x, axis=-1), ctx_1024, L0_xattn_W_reduce, L0_xattn_b_reduce)
    x = x + jnp.tanh(g_ffn[0]) * _L0_ffn_ref(_layernorm(x, axis=-1), L0_ffn_kernel, L0_ffn_input_scale, L0_ffn_kernel_scale, L0_ffn_bias)
    return x

_drawn_inputs = setup_inputs


def setup_inputs(seed=0):
    import zlib

    import numpy as np

    out = dict(_drawn_inputs(seed))
    spreads = {'L0_ffn_bias': (0.0, 0.1)}
    factors = {}
    for name, (base, spread) in spreads.items():
        noise = np.random.default_rng([zlib.crc32(name.encode()), seed]).standard_normal(out[name].shape)
        drawn = base * np.exp(spread * noise) if base else spread * noise
        out[name] = jnp.asarray(drawn.astype(out[name].dtype))
    for name, factor in factors.items():
        out[name] = (out[name] * factor).astype(out[name].dtype)
    return out
```

```python
from contextlib import ExitStack

import concourse.bass as bass
from concourse import mybir

F32 = mybir.dt.float32
BF16 = mybir.dt.bfloat16
FP8 = mybir.dt.float8e4
I32 = mybir.dt.int32
ALU = mybir.AluOpType
ACT = mybir.ActivationFunctionType

P = 128
WINDOW = 20
EPS = 1e-5
OUTSIDE = 1e30
ROUND_4_BITS = 1.5 * 2.0 ** 20
E4M3_LEAST_NORMAL = 2.0 ** -6
E4M3_LARGEST = 448.0


def flamingo_block(nc, x, x_t, ctx, ctx_t, w_t, b_col, b_row, w_ffn, bias_ffn, scalars, out):
    D = 256
    DC = D // P
    PAIR = 2 * D
    PAIRS = x.shape[1] // PAIR
    NB = 2
    assert x.shape[0] == P and PAIRS >= 8 and PAIRS % 2 == 0

    with ExitStack() as stack:
        def sb(name, shape, dt=F32):
            return stack.enter_context(nc.sbuf_tensor(name, shape, dt))

        def bank(name, shape, dt=F32):
            return stack.enter_context(nc.psum_tensor(name, shape, dt))

        def sem(name):
            return stack.enter_context(nc.semaphore(name))

        x_sb = sb("x_sb", [P, PAIRS * PAIR])
        ctx_sb = sb("ctx_sb", [P, PAIRS * PAIR])
        ctxt_sb = sb("ctxt_sb", [P, PAIRS * PAIR])
        xt_sb = sb("xt_sb", [P, 2, DC, NB, P])
        keys_sb = sb("keys_sb", [P, 2, DC, NB, P])
        neg_sb = sb("neg_sb", [P, 2, NB, P])
        probs_sb = sb("probs_sb", [P, 2, NB, P])
        probst_sb = sb("probst_sb", [P, 2, NB, P])
        normed_sb = sb("normed_sb", [P, 2, NB, DC, P], BF16)
        quant_sb = sb("quant_sb", [P, 2, NB, DC, P], FP8)
        wide_sb = sb("wide_sb", [P, 2, NB, DC, P], BF16)
        y_sb = sb("y_sb", [P, 2, NB, D], BF16)
        negmin_sb = sb("negmin_sb", [P, 2, NB])
        rowsum_sb = sb("rowsum_sb", [P, 2, NB])
        recip_sb = sb("recip_sb", [P, 2, NB])
        gate_sb = sb("gate_sb", [P, 2, NB])
        bn1_sb = sb("bn1_sb", [P, 2, NB, 6])
        mv1_sb = sb("mv1_sb", [P, 2, NB, 2])
        var1_sb = sb("var1_sb", [P, 2, NB])
        rstd1_sb = sb("rstd1_sb", [P, 2, NB])
        bn2_sb = sb("bn2_sb", [P, 2, NB, 6])
        mv2_sb = sb("mv2_sb", [P, 2, NB, 2])
        var2_sb = sb("var2_sb", [P, 2, NB])
        negmean2_sb = sb("negmean2_sb", [P, 2, NB])
        rstd2_sb = sb("rstd2_sb", [P, 2, NB])
        w_sb = sb("w_sb", [P, DC, D])
        wc_sb = sb("wc_sb", [P, DC, D])
        wstat_sb = sb("wstat_sb", [P, DC + 1, 6])
        wmean_sb = sb("wmean_sb", [P, DC + 1, 2])
        bcol_sb = sb("bcol_sb", [P, DC])
        brow_sb = sb("brow_sb", [P, D])
        bc_sb = sb("bc_sb", [P, DC])
        wf_sb = sb("wf_sb", [P, DC * D], BF16)
        wq_sb = sb("wq_sb", [P, DC, D], BF16)
        bias_sb = sb("bias_sb", [P, NB, D], BF16)
        scal_sb = sb("scal_sb", [P, 4])
        tanh_sb = sb("tanh_sb", [P, 2])
        inv_sb = sb("inv_sb", [P, 2])
        prod_sb = sb("prod_sb", [P, 1])
        half_sb = sb("half_sb", [P, NB])
        band_sb = sb("band_sb", [P, P])
        ident_sb = sb("ident_sb", [P, P])
        identb_sb = sb("identb_sb", [P, P], BF16)
        r_u = sb("r_u", [P, PAIR])
        r_m = sb("r_m", [P, PAIR])
        r_q = sb("r_q", [P, PAIR])

        keys_ps = bank("keys_ps", [P, DC, NB * P])
        scores_ps = [bank(f"scores_ps{h}", [P, 512]) for h in range(NB)]
        probst_ps = bank("probst_ps", [P, 4, P])
        attn_ps = [bank(f"attn_ps{h}", [P, 512]) for h in range(NB)]
        normedt_ps = bank("normedt_ps", [P, 2 * NB, DC, P], BF16)
        ffn_ps = bank("ffn_ps", [P, NB, D])

        x_landed = [sem("x_landed0"), sem("x_landed1")]
        xt_landed = [sem("xt_landed0"), sem("xt_landed1")]
        ctx_landed = [sem("ctx_landed0"), sem("ctx_landed1")]
        ctxt_landed = [sem("ctxt_landed0"), sem("ctxt_landed1")]
        w_landed = sem("w_landed")
        b_landed = sem("b_landed")
        scalars_landed = sem("scalars_landed")
        ffn_landed = sem("ffn_landed")
        stored = sem("stored")
        pool_step = sem("pool_step")
        consts_made = sem("consts_made")
        tanh_made = sem("tanh_made")
        inv_made = sem("inv_made")
        w_centred = sem("w_centred")
        dve_step = sem("dve_step")
        wq_made = sem("wq_made")
        keys_done = sem("keys_done")
        keys_copied = sem("keys_copied")
        scores_done = sem("scores_done")
        masked = sem("masked")
        probs_done = sem("probs_done")
        probst_done = sem("probst_done")
        probst_copied = sem("probst_copied")
        attn_done = sem("attn_done")
        recip_done = sem("recip_done")
        gate_done = sem("gate_done")
        resid_done = sem("resid_done")
        bn1_done = sem("bn1_done")
        stats1_done = sem("stats1_done")
        var1_done = sem("var1_done")
        rstd1_done = sem("rstd1_done")
        bn2_done = sem("bn2_done")
        stats2_done = sem("stats2_done")
        var2_done = sem("var2_done")
        rstd2_done = sem("rstd2_done")
        normed = sem("normed")
        normedt_done = sem("normedt_done")
        quantized = sem("quantized")
        ffn_done = sem("ffn_done")
        y_copied = sem("y_copied")
        y_biased = sem("y_biased")
        result_done = sem("result_done")

        block = stack.enter_context(nc.Block())

        def landed_count(p, parity):
            return (p - parity) * 8 + 16

        def run(engine, step, first, last, lo, hi):
            for i in range(first, lo):
                step(i, i % 2)
            for i in range(lo, hi, 2):
                step(i, lo % 2, full=True)
                step(i + 1, (lo + 1) % 2, full=True)
            for i in range(hi, last + 1):
                step(i, i % 2)

        def cols(p, start, size):
            return bass.ds(p * PAIR + start, size)

        @block.sync
        def _(sp):
            def load(p, parity, first=False):
                for dst, src, landed in ((ctxt_sb, ctx_t, ctxt_landed), (x_sb, x, x_landed), (ctx_sb, ctx, ctx_landed)):
                    if not first:
                        sp.wait_ge(landed[parity], landed_count(p - 2, parity))
                    sp.dma_start(dst[:, cols(p, 0, PAIR)], src[:, cols(p, 0, PAIR)]).then_inc(landed[parity], 16)
                    if dst is ctxt_sb:
                        if not first:
                            sp.wait_ge(scores_done, (p - 2) * NB + NB)
                        sp.dma_start(xt_sb[:, parity].rearrange("p c b r -> p (c b r)"),
                                     x_t[:, cols(p, 0, PAIR)]).then_inc(xt_landed[parity], 16)

            def store(p):
                sp.wait_ge(result_done, p * NB + NB)
                sp.dma_start(out[:, cols(p, 0, PAIR)], x_sb[:, cols(p, 0, PAIR)]).then_inc(stored, 16)

            def step(i, parity, full=False):
                if full or i + 2 < PAIRS:
                    load(i + 2, parity)
                if full or i >= 2:
                    store(i - 2)

            sp.dma_start(w_sb[:, :, :].rearrange("p c o -> p (c o)"), w_t).then_inc(w_landed, 16)
            load(0, 0, first=True)
            load(1, 1, first=True)
            run(sp, step, 0, PAIRS + 1, 2, 6)
            sp.wait_ge(stored, 16 * PAIRS)

        @block.gpsimd
        def _(pool):
            made = [0]

            def link(ins):
                made[0] += 1
                ins.then_inc(pool_step, 1)
                pool.wait_ge(pool_step, made[0])

            link(nc.gpsimd.memset(ident_sb[:, :], 0.0))
            link(nc.gpsimd.affine_select(out=ident_sb[:, :], in_=ident_sb[:, :], compare_op=ALU.not_equal, fill=1.0,
                                         base=0, pattern=[[-1, P]], channel_multiplier=1))
            link(nc.gpsimd.memset(half_sb[:, :], -0.5))
            link(nc.gpsimd.memset(band_sb[:, :], 0.0))
            link(nc.gpsimd.affine_select(out=band_sb[:, :], in_=band_sb[:, :], compare_op=ALU.is_ge, fill=OUTSIDE,
                                         base=WINDOW, pattern=[[-1, P]], channel_multiplier=1))
            link(nc.gpsimd.affine_select(out=band_sb[:, :], in_=band_sb[:, :], compare_op=ALU.is_ge, fill=OUTSIDE,
                                         base=WINDOW, pattern=[[1, P]], channel_multiplier=-1))
            nc.gpsimd.tensor_copy(identb_sb[:, :], ident_sb[:, :]).then_inc(consts_made, 1)

            def rstd1(p, s):
                pool.wait_ge(stats1_done, p * NB + NB)
                nc.gpsimd.tensor_scalar(var1_sb[:, s, :], mv1_sb[:, s, :, 1], 1.0, EPS,
                                        ALU.mult, ALU.add).then_inc(var1_done, 1)
                pool.wait_ge(var1_done, p + 1)
                nc.gpsimd.tensor_tensor(rstd1_sb[:, s, :], var1_sb[:, s, :], half_sb[:, :],
                                        ALU.pow).then_inc(rstd1_done, 1)

            def norm2(p, s):
                pool.wait_ge(stats2_done, p * NB + NB)
                nc.gpsimd.tensor_scalar(var2_sb[:, s, :], mv2_sb[:, s, :, 1], 1.0, EPS,
                                        ALU.mult, ALU.add).then_inc(var2_done, 1)
                nc.gpsimd.tensor_scalar(negmean2_sb[:, s, :], mv2_sb[:, s, :, 0], -1.0, 0.0,
                                        ALU.mult, ALU.add).then_inc(var2_done, 1)
                pool.wait_ge(var2_done, p * 2 + 2)
                nc.gpsimd.tensor_tensor(rstd2_sb[:, s, :], var2_sb[:, s, :], half_sb[:, :],
                                        ALU.pow).then_inc(rstd2_done, 1)
                pool.wait_ge(rstd2_done, p + 1)
                for h in range(NB):
                    nc.gpsimd.tensor_scalar(normed_sb[:, s, h].rearrange("p c r -> p (c r)"), x_sb[:, cols(p, h * D, D)],
                                            negmean2_sb[:, s, h:h + 1], rstd2_sb[:, s, h:h + 1],
                                            ALU.add, ALU.mult).then_inc(normed, 1)

            def step(i, parity, full=False):
                if full or 0 <= i - 1 < PAIRS:
                    norm2(i - 1, 1 - parity)
                if full or i + 1 < PAIRS:
                    rstd1(i + 1, 1 - parity)

            rstd1(0, 0)
            run(pool, step, 0, PAIRS, 2, 6)

        @block.scalar
        def _(act):
            act.dma_start(scal_sb[:, :], scalars.partition_broadcast(P)).then_inc(scalars_landed, 16)
            act.dma_start(bcol_sb[:, :], b_col).then_inc(b_landed, 16)
            act.dma_start(brow_sb[:, :], b_row.partition_broadcast(P)).then_inc(b_landed, 16)
            act.dma_start(wf_sb[:, :], w_ffn).then_inc(ffn_landed, 16)
            for h in range(NB):
                act.dma_start(bias_sb[:, h, :], bias_ffn.partition_broadcast(P)).then_inc(ffn_landed, 16)
            act.wait_ge(scalars_landed, 16)
            nc.scalar.activation(tanh_sb[:, :], scal_sb[:, 0:2], ACT.Tanh).then_inc(tanh_made, 1)

            def copy_keys(p, s):
                act.wait_ge(keys_done, p + 1)
                for c in range(DC):
                    ins = nc.scalar.activation(keys_sb[:, s, c].rearrange("p b k -> p (b k)"), keys_ps[:, c, :],
                                               ACT.Identity, bias=bc_sb[:, c:c + 1])
                ins.then_inc(keys_copied, 1)

            def softmax(p, s):
                for h in range(NB):
                    act.wait_ge(masked, p * NB + h + 1)
                    nc.scalar.activation(probs_sb[:, s, h], neg_sb[:, s, h], ACT.Exp, bias=negmin_sb[:, s, h:h + 1],
                                         scale=-1.0, accum_out=rowsum_sb[:, s, h:h + 1]).then_inc(probs_done, 1)

            def copy_probst(p, s):
                act.wait_ge(probst_done, p + 1)
                nc.scalar.copy(probst_sb[:, s], probst_ps[:, 0:NB, :]).then_inc(probst_copied, 1)

            def quantize(p, s):
                act.wait_ge(normedt_done, p + 1)
                if p is 0:
                    act.wait_ge(inv_made, 1)
                nc.scalar.activation(quant_sb[:, s].rearrange("p b c r -> p (b c r)"),
                                     normedt_ps[:, 0:NB].rearrange("p b c r -> p (b c r)"), ACT.Copy,
                                     scale=inv_sb[:, 0:1], saturate=False).then_inc(quantized, 1)

            def copy_y(p, s):
                act.wait_ge(ffn_done, p + 1)
                nc.scalar.activation(y_sb[:, s], ffn_ps[:, :, :], ACT.Copy, scale=prod_sb[:, 0:1]).then_inc(y_copied, 1)

            def step(i, parity, full=False):
                if full or i < PAIRS:
                    softmax(i, parity)
                if full or i >= 2:
                    copy_y(i - 2, parity)
                if full or i < PAIRS:
                    copy_probst(i, parity)
                if full or i + 1 < PAIRS:
                    copy_keys(i + 1, 1 - parity)
                if full or 0 <= i - 1 < PAIRS:
                    quantize(i - 1, 1 - parity)

            act.wait_ge(w_centred, 1)
            copy_keys(0, 0)
            run(act, step, 0, PAIRS + 1, 2, 6)

        @block.vector
        def _(dve):
            made = [0]

            def link(ins):
                made[0] += 1
                ins.then_inc(dve_step, 1)
                dve.wait_ge(dve_step, made[0])

            def centre_weights():
                dve.wait_ge(w_landed, 16)
                for c in range(DC):
                    nc.vector.bn_stats(wstat_sb[:, c, :], w_sb[:, c, :])
                dve.wait_ge(b_landed, 32)
                link(nc.vector.bn_stats(wstat_sb[:, DC, :], brow_sb[:, :]))
                for c in range(DC + 1):
                    ins = nc.vector.bn_aggr(wmean_sb[:, c, :], wstat_sb[:, c, :])
                link(ins)
                for c in range(DC):
                    nc.vector.tensor_scalar(wc_sb[:, c, :], w_sb[:, c, :], wmean_sb[:, c, 0:1], -1.0,
                                            ALU.subtract, ALU.mult)
                nc.vector.tensor_scalar(bc_sb[:, :], bcol_sb[:, :], wmean_sb[:, DC, 0:1], -1.0,
                                        ALU.subtract, ALU.mult).then_inc(w_centred, 1)

            def scales():
                dve.wait_ge(scalars_landed, 16)
                nc.vector.tensor_scalar(prod_sb[:, :], scal_sb[:, 2:3], scal_sb[:, 3:4], None, ALU.mult)
                link(nc.vector.reciprocal(inv_sb[:, :], scal_sb[:, 2:4]))

            def round_e4m3fn(dst, src, scale):
                link(nc.vector.tensor_scalar(r_u[:, :], src, scale, None, ALU.mult))
                link(nc.vector.tensor_scalar(r_m[:, :].bitcast(I32), r_u[:, :].bitcast(I32), 0x7F800000, None,
                                             ALU.bitwise_and))
                link(nc.vector.tensor_scalar(r_m[:, :], r_m[:, :], E4M3_LEAST_NORMAL, ROUND_4_BITS, ALU.max, ALU.mult))
                link(nc.vector.tensor_tensor(r_q[:, :], r_u[:, :], r_m[:, :], ALU.add))
                link(nc.vector.tensor_tensor(r_q[:, :], r_q[:, :], r_m[:, :], ALU.subtract))
                link(nc.vector.tensor_tensor(r_u[:, :], r_q[:, :], r_q[:, :], ALU.mult))
                link(nc.vector.tensor_scalar(r_u[:, :], r_u[:, :], E4M3_LARGEST ** 2, 3e38, ALU.is_gt, ALU.mult))
                link(nc.vector.tensor_tensor(r_u[:, :], r_u[:, :], r_u[:, :], ALU.add))
                link(nc.vector.tensor_tensor(r_u[:, :], r_u[:, :], r_u[:, :], ALU.subtract))
                return nc.vector.tensor_tensor(dst, r_q[:, :], r_u[:, :], ALU.add)

            def bn1(p, s, h):
                if h == 0:
                    dve.wait_ge(x_landed[s], landed_count(p, s))
                nc.vector.bn_stats(bn1_sb[:, s, h, :], x_sb[:, cols(p, h * D, D)]).then_inc(bn1_done, 1)

            def aggr1(p, s):
                dve.wait_ge(bn1_done, p * NB + NB)
                for h in range(NB):
                    nc.vector.bn_aggr(mv1_sb[:, s, h, :], bn1_sb[:, s, h, :]).then_inc(stats1_done, 1)

            def mask(p, s):
                dve.wait_ge(rstd1_done, p + 1)
                for h in range(NB):
                    dve.wait_ge(scores_done, p * NB + h + 1)
                    nc.vector.tensor_tensor_reduce(neg_sb[:, s, h], scores_ps[h][:, 0:P], band_sb[:, :],
                                                   rstd1_sb[:, s, h:h + 1], 3e38, ALU.add, ALU.min,
                                                   negmin_sb[:, s, h:h + 1]).then_inc(masked, 1)

            def residual(p, s):
                dve.wait_ge(gate_done, p + 1)
                for h in range(NB):
                    dve.wait_ge(attn_done, p * NB + h + 1)
                    xs = x_sb[:, cols(p, h * D, D)]
                    nc.vector.scalar_tensor_tensor(out=xs, in0=attn_ps[h][:, 0:D], scalar=gate_sb[:, s, h:h + 1], in1=xs,
                                                   op0=ALU.mult, op1=ALU.add).then_inc(resid_done, 1)

            def bn2(p, s):
                for h in range(NB):
                    dve.wait_ge(resid_done, p * NB + h + 1)
                    nc.vector.bn_stats(bn2_sb[:, s, h, :], x_sb[:, cols(p, h * D, D)]).then_inc(bn2_done, 1)

            def aggr2(p, s):
                dve.wait_ge(bn2_done, p * NB + NB)
                for h in range(NB):
                    nc.vector.bn_aggr(mv2_sb[:, s, h, :], bn2_sb[:, s, h, :]).then_inc(stats2_done, 1)

            def reciprocal(p, s):
                dve.wait_ge(probs_done, p * NB + NB)
                nc.vector.reciprocal(recip_sb[:, s, :], rowsum_sb[:, s, :]).then_inc(recip_done, 1)

            def gate(p, s):
                dve.wait_ge(recip_done, p + 1)
                nc.vector.tensor_scalar(gate_sb[:, s, :], recip_sb[:, s, :], tanh_sb[:, 0:1], None,
                                        ALU.mult).then_inc(gate_done, 1)

            def add_bias(p, s):
                dve.wait_ge(y_copied, p + 1)
                nc.vector.tensor_tensor(y_sb[:, s], y_sb[:, s], bias_sb[:, :, :], ALU.add).then_inc(y_biased, 1)

            def result(p, s):
                dve.wait_ge(y_biased, p + 1)
                for h in range(NB):
                    xs = x_sb[:, cols(p, h * D, D)]
                    nc.vector.scalar_tensor_tensor(out=xs, in0=y_sb[:, s, h], scalar=tanh_sb[:, 1:2], in1=xs,
                                                   op0=ALU.mult, op1=ALU.add).then_inc(result_done, 1)

            def step(i, parity, full=False):
                other = 1 - parity
                if full or 0 <= i - 1 < PAIRS:
                    residual(i - 1, other)
                if full or i < PAIRS:
                    mask(i, parity)
                if full or 0 <= i - 1 < PAIRS:
                    bn2(i - 1, other)
                if full or i + 1 < PAIRS:
                    bn1(i + 1, other, 0)
                if full or 0 <= i - 1 < PAIRS:
                    aggr2(i - 1, other)
                if full or i + 1 < PAIRS:
                    bn1(i + 1, other, 1)
                if full or i < PAIRS:
                    reciprocal(i, parity)
                if full or i + 1 < PAIRS:
                    aggr1(i + 1, other)
                if full or i < PAIRS:
                    gate(i, parity)
                if full or i >= 2:
                    add_bias(i - 2, parity)
                    result(i - 2, parity)
                if i is 0:
                    dve.wait_ge(ffn_landed, 48)
                    round_e4m3fn(wq_sb[:, :, :].rearrange("p c f -> p (c f)"), wf_sb[:, :],
                                 inv_sb[:, 1:2]).then_inc(wq_made, 1)

            centre_weights()
            scales()
            nc.vector.memset(r_u[:, 0:1], 0.0).then_inc(inv_made, 1)
            bn1(0, 0, 0)
            bn1(0, 0, 1)
            aggr1(0, 0)
            dve.wait_ge(tanh_made, 1)
            dve.wait_ge(consts_made, 1)
            run(dve, step, 0, PAIRS + 1, 2, 6)

        @block.tensor
        def _(pe):
            def keys(p, s, o):
                if o == 0:
                    pe.wait_ge(ctxt_landed[s], landed_count(p, s))
                    if p is not 0:
                        pe.wait_ge(keys_copied, p)
                for c in range(DC):
                    ins = nc.tensor.matmul(keys_ps[:, o, :], wc_sb[:, c, o * P:(o + 1) * P],
                                           ctxt_sb[:, cols(p, c * NB * P, NB * P)],
                                           start=(c == 0), stop=(c == DC - 1))
                if o == DC - 1:
                    ins.then_inc(keys_done, 1)

            def scores(p, s):
                pe.wait_ge(xt_landed[s], landed_count(p, s))
                pe.wait_ge(keys_copied, p + 1)
                if p is not 0:
                    pe.wait_ge(masked, p * NB)
                for h in range(NB):
                    for c in range(DC):
                        ins = nc.tensor.matmul(scores_ps[h][:, 0:P], xt_sb[:, s, c, h, :], keys_sb[:, s, c, h, :],
                                               start=(c == 0), stop=(c == DC - 1))
                    ins.then_inc(scores_done, 1)

            def transpose_probs(p, s):
                pe.wait_ge(probs_done, p * NB + NB)
                if p is not 0:
                    pe.wait_ge(probst_copied, p)
                for h in range(NB):
                    ins = nc.tensor.transpose(probst_ps[:, h, :], probs_sb[:, s, h], ident_sb[:, :])
                ins.then_inc(probst_done, 1)

            def attend(p, s):
                pe.wait_ge(ctx_landed[s], landed_count(p, s))
                pe.wait_ge(probst_copied, p + 1)
                if p is not 0:
                    pe.wait_ge(resid_done, p * NB)
                for h in range(NB):
                    nc.tensor.matmul(attn_ps[h][:, 0:D], probst_sb[:, s, h], ctx_sb[:, cols(p, h * D, D)],
                                     start=True, stop=True).then_inc(attn_done, 1)

            def transpose_normed(p, s):
                pe.wait_ge(normed, p * NB + NB)
                if p is not 0:
                    pe.wait_ge(quantized, p)
                for h in range(NB):
                    for c in range(DC):
                        ins = nc.tensor.transpose(normedt_ps[:, h, c, :], normed_sb[:, s, h, c, :], identb_sb[:, :])
                ins.then_inc(normedt_done, 1)

            def ffn(p, s):
                pe.wait_ge(quantized, p + 1)
                if p is 0:
                    pe.wait_ge(wq_made, 1)
                else:
                    pe.wait_ge(y_copied, p)
                for h in range(NB):
                    for c in range(DC):
                        ins = nc.tensor.matmul(ffn_ps[:, h, :], quant_sb[:, s, h, c, :], wq_sb[:, c, :],
                                               start=(c == 0), stop=(c == DC - 1))
                ins.then_inc(ffn_done, 1)

            def step(i, parity, full=False):
                if full or i < PAIRS:
                    scores(i, parity)
                if full or i >= 2:
                    ffn(i - 2, parity)
                if full or i + 1 < PAIRS:
                    keys(i + 1, 1 - parity, 0)
                if full or i < PAIRS:
                    transpose_probs(i, parity)
                if full or i + 1 < PAIRS:
                    keys(i + 1, 1 - parity, 1)
                if full or i < PAIRS:
                    attend(i, parity)
                if full or 0 <= i - 1 < PAIRS:
                    transpose_normed(i - 1, 1 - parity)

            pe.wait_ge(w_centred, 1)
            for o in range(DC):
                keys(0, 0, o)
            pe.wait_ge(consts_made, 1)
            run(pe, step, 0, PAIRS + 1, 2, 6)


def kernel(x, ctx_1024, g_xattn, g_ffn, L0_xattn_W_reduce, L0_xattn_b_reduce, L0_ffn_kernel, L0_ffn_input_scale,
           L0_ffn_kernel_scale, L0_ffn_bias):
    import numpy as np
    import concourse.bacc as bacc
    from concourse.bass_utils import run_bass_kernel_spmd

    x, ctx, w, wf = (np.asarray(a) for a in (x, ctx_1024, L0_xattn_W_reduce, L0_ffn_kernel))
    B, S, D = x.shape
    chunks = D // P

    def rows(a):
        return np.ascontiguousarray(a.transpose(1, 0, 2).reshape(S, B * D))

    def features(a):
        return np.ascontiguousarray(a.reshape(B // 2, 2, S, chunks, P).transpose(4, 0, 3, 1, 2).reshape(P, B * D))

    arrays = {
        "x": rows(x),
        "x_t": features(x),
        "ctx": rows(ctx),
        "ctx_t": features(ctx),
        "w_t": np.ascontiguousarray(w.T.reshape(chunks, P, D).transpose(1, 0, 2).reshape(P, chunks * D)),
        "b_col": np.ascontiguousarray(np.asarray(L0_xattn_b_reduce).reshape(chunks, P).T),
        "b_row": np.asarray(L0_xattn_b_reduce),
        "w_ffn": np.ascontiguousarray(wf.reshape(chunks, P, D).transpose(1, 0, 2).reshape(P, chunks * D)),
        "bias_ffn": np.asarray(L0_ffn_bias),
        "scalars": np.concatenate([np.asarray(a) for a in (g_xattn, g_ffn, L0_ffn_input_scale, L0_ffn_kernel_scale)]),
    }
    nc = bacc.Bacc("TRN2", target_bir_lowering=False, num_devices=1)
    args = [nc.dram_tensor(f"in_{name}", a.shape, mybir.dt.from_np(a.dtype), kind="ExternalInput").ap()
            for name, a in arrays.items()]
    out = nc.dram_tensor("out", (S, B * D), F32, kind="ExternalOutput").ap()
    flamingo_block(nc, *args, out)
    r = run_bass_kernel_spmd(nc, [{f"in_{name}": a for name, a in arrays.items()}], core_ids=[0])
    got = r.results[0]["out"]
    return np.ascontiguousarray(got.reshape(S, B, D).transpose(1, 0, 2))
```

```python
from contextlib import ExitStack

import concourse.bass as bass
from concourse import mybir

F32 = mybir.dt.float32
BF16 = mybir.dt.bfloat16
FP8 = mybir.dt.float8e4
I32 = mybir.dt.int32
ALU = mybir.AluOpType
ACT = mybir.ActivationFunctionType

P = 128
WINDOW = 20
EPS = 1e-5
OUTSIDE = 1e30
ROUND_4_BITS = 1.5 * 2.0 ** 20
E4M3_LEAST_NORMAL = 2.0 ** -6
E4M3_LARGEST = 448.0
WARM_UP = 8


def flamingo_block(nc, x, x_t, ctx, ctx_t, w_t, small, ffn_consts, out):
    D = 256
    DC = D // P
    PAIR = 2 * D
    PAIRS = x.shape[1] // PAIR
    NB = 2
    LAST = PAIRS - 1
    assert x.shape[0] == P and PAIRS >= 8 and PAIRS % 2 == 0

    with ExitStack() as stack:
        def sb(name, shape, dt=F32):
            return stack.enter_context(nc.sbuf_tensor(name, shape, dt))

        def bank(name, shape, dt=F32):
            return stack.enter_context(nc.psum_tensor(name, shape, dt))

        def sem(name):
            return stack.enter_context(nc.semaphore(name))

        x_sb = sb("x_sb", [P, PAIRS * PAIR])
        ctx_sb = sb("ctx_sb", [P, PAIRS * PAIR])
        ctxt_sb = sb("ctxt_sb", [P, PAIRS * PAIR])
        xt_sb = sb("xt_sb", [P, 2, DC, NB, P])
        keys_sb = sb("keys_sb", [P, 2, DC, NB, P])
        neg_sb = sb("neg_sb", [P, 2, NB, P])
        probs_sb = sb("probs_sb", [P, 2, NB, P])
        probst_sb = sb("probst_sb", [P, 2, NB, P])
        normed_sb = sb("normed_sb", [P, 2, NB, DC, P], BF16)
        quant_sb = sb("quant_sb", [P, 2, NB, DC, P], FP8)
        wide_sb = sb("wide_sb", [P, 2, NB, DC, P], BF16)
        y_sb = sb("y_sb", [P, 2, NB, D], BF16)
        negmin_sb = sb("negmin_sb", [P, 2, NB])
        rowsum_sb = sb("rowsum_sb", [P, 2, NB])
        recip_sb = sb("recip_sb", [P, 2, NB])
        gate_sb = sb("gate_sb", [P, 2, NB])
        bn1_sb = sb("bn1_sb", [P, 2, NB, 6])
        mv1_sb = sb("mv1_sb", [P, 2, NB, 2])
        var1_sb = sb("var1_sb", [P, 2, NB])
        rstd1_sb = sb("rstd1_sb", [P, 2, NB])
        bn2_sb = sb("bn2_sb", [P, 2, NB, 6])
        mv2_sb = sb("mv2_sb", [P, 2, NB, 2])
        var2_sb = sb("var2_sb", [P, 2, NB])
        negmean2_sb = sb("negmean2_sb", [P, 2, NB])
        rstd2_sb = sb("rstd2_sb", [P, 2, NB])
        w_sb = sb("w_sb", [P, DC, D])
        wc_sb = sb("wc_sb", [P, DC, D])
        wstat_sb = sb("wstat_sb", [P, DC + 1, 6])
        wmean_sb = sb("wmean_sb", [P, DC + 1, 2])
        small_sb = sb("small_sb", [P, 4 + DC + D])
        scal_sb = small_sb[:, 0:4]
        bcol_sb = small_sb[:, 4:4 + DC]
        brow_sb = small_sb[:, 4 + DC:4 + DC + D]
        bc_sb = sb("bc_sb", [P, DC])
        ffnc_sb = sb("ffnc_sb", [P, (DC + NB) * D], BF16)
        wf_sb = ffnc_sb[:, 0:DC * D]
        bias_sb = ffnc_sb[:, DC * D:(DC + NB) * D].rearrange("p (b f) -> p b f", b=NB)
        wq_sb = sb("wq_sb", [P, DC, D], BF16)
        tanh_sb = sb("tanh_sb", [P, 2])
        inv_sb = sb("inv_sb", [P, 2])
        prod_sb = sb("prod_sb", [P, 1])
        half_sb = sb("half_sb", [P, NB])
        band_sb = sb("band_sb", [P, P])
        ident_sb = sb("ident_sb", [P, P])
        identb_sb = sb("identb_sb", [P, P], BF16)
        r_u = sb("r_u", [P, PAIR])
        r_m = sb("r_m", [P, PAIR])
        r_q = sb("r_q", [P, PAIR], BF16)
        r_c = sb("r_c", [P, PAIR], BF16)
        warm_sb = sb("warm_sb", [P, PAIR], BF16)

        keys_ps = bank("keys_ps", [P, DC, NB * P])
        scores_ps = [bank(f"scores_ps{h}", [P, 512]) for h in range(NB)]
        probst_ps = bank("probst_ps", [P, 4, P])
        attn_ps = [bank(f"attn_ps{h}", [P, 512]) for h in range(NB)]
        normedt_ps = bank("normedt_ps", [P, 2 * NB, DC, P], BF16)
        ffn_ps = bank("ffn_ps", [P, NB, D])

        def normedt_at(p, h):
            if p is LAST and h == 1:
                return scores_ps[1][:, 0:P].bitcast(BF16).rearrange("p (c r) -> p c r", c=DC)
            return normedt_ps[:, h]

        def ffn_at(p, h):
            return scores_ps[0][:, 0:D] if p is LAST and h == 1 else ffn_ps[:, h, :]

        x_landed = [sem("x_landed0"), sem("x_landed1")]
        xt_landed = [sem("xt_landed0"), sem("xt_landed1")]
        ctx_landed = [sem("ctx_landed0"), sem("ctx_landed1")]
        ctxt_landed = [sem("ctxt_landed0"), sem("ctxt_landed1")]
        w_landed = sem("w_landed")
        small_landed = sem("small_landed")
        ffn_landed = sem("ffn_landed")
        stored = sem("stored")
        pool_step = sem("pool_step")
        consts_made = sem("consts_made")
        tanh_made = sem("tanh_made")
        scales_made = sem("scales_made")
        w_centred = sem("w_centred")
        b_centred = sem("b_centred")
        zeros_made = sem("zeros_made")
        dve_step = sem("dve_step")
        wq_made = sem("wq_made")
        keys_done = sem("keys_done")
        keys_copied = sem("keys_copied")
        scores_done = sem("scores_done")
        masked = sem("masked")
        probs_done = sem("probs_done")
        probst_done = sem("probst_done")
        probst_copied = sem("probst_copied")
        attn_done = sem("attn_done")
        recip_done = sem("recip_done")
        gate_done = sem("gate_done")
        resid_done = sem("resid_done")
        bn1_done = sem("bn1_done")
        stats1_done = sem("stats1_done")
        var1_done = sem("var1_done")
        rstd1_done = sem("rstd1_done")
        bn2_done = sem("bn2_done")
        stats2_done = sem("stats2_done")
        var2_done = sem("var2_done")
        rstd2_done = sem("rstd2_done")
        var2_last = sem("var2_last")
        normed = sem("normed")
        normedt_done = sem("normedt_done")
        quantized = sem("quantized")
        ffn_done = sem("ffn_done")
        y_copied = sem("y_copied")
        y_biased = sem("y_biased")
        result_done = sem("result_done")

        block = stack.enter_context(nc.Block())

        def landed_count(p, parity):
            return (p - parity) * 8 + 16

        def run(engine, step, first, last, lo, hi):
            for i in range(first, lo):
                step(i, i % 2)
            for i in range(lo, hi, 2):
                step(i, lo % 2, full=True)
                step(i + 1, (lo + 1) % 2, full=True)
            for i in range(hi, last + 1):
                step(i, i % 2)

        def cols(p, start, size):
            return bass.ds(p * PAIR + start, size)

        @block.sync
        def _(sp):
            def load(p, parity, first=False):
                for dst, src, landed in ((ctxt_sb, ctx_t, ctxt_landed), (x_sb, x, x_landed), (ctx_sb, ctx, ctx_landed)):
                    if not first:
                        sp.wait_ge(landed[parity], landed_count(p - 2, parity))
                    sp.dma_start(dst[:, cols(p, 0, PAIR)], src[:, cols(p, 0, PAIR)]).then_inc(landed[parity], 16)
                    if dst is ctxt_sb:
                        if not first:
                            sp.wait_ge(scores_done, (p - 2) * NB + NB)
                        sp.dma_start(xt_sb[:, parity].rearrange("p c b r -> p (c b r)"),
                                     x_t[:, cols(p, 0, PAIR)]).then_inc(xt_landed[parity], 16)

            def store(p):
                sp.wait_ge(result_done, p * NB + NB)
                sp.dma_start(out[:, cols(p, 0, PAIR)], x_sb[:, cols(p, 0, PAIR)]).then_inc(stored, 16)

            def store_last(h):
                sp.wait_ge(result_done, LAST * NB + h + 1)
                sp.dma_start(out[:, cols(LAST, h * D, D)], x_sb[:, cols(LAST, h * D, D)]).then_inc(stored, 16)

            def step(i, parity, full=False):
                if full or i + 2 < PAIRS:
                    load(i + 2, parity)
                if full or i >= 3:
                    store(i - 3)

            sp.dma_start(w_sb[:, :, :].rearrange("p c o -> p (c o)"), w_t).then_inc(w_landed, 16)
            sp.dma_start(small_sb[:, :], small).then_inc(small_landed, 16)
            load(0, 0, first=True)
            sp.dma_start(ffnc_sb[:, :], ffn_consts).then_inc(ffn_landed, 16)
            load(1, 1, first=True)
            run(sp, step, 0, PAIRS + 1, 3, 5)
            for h in range(NB):
                store_last(h)
            sp.wait_ge(stored, 16 * (LAST + NB))

        @block.gpsimd
        def _(pool):
            made = [0]

            def link(ins):
                made[0] += 1
                ins.then_inc(pool_step, 1)
                pool.wait_ge(pool_step, made[0])

            link(nc.gpsimd.memset(ident_sb[:, :], 0.0))
            link(nc.gpsimd.affine_select(out=ident_sb[:, :], in_=ident_sb[:, :], compare_op=ALU.not_equal, fill=1.0,
                                         base=0, pattern=[[-1, P]], channel_multiplier=1))
            link(nc.gpsimd.memset(half_sb[:, :], -0.5))
            link(nc.gpsimd.memset(band_sb[:, :], 0.0))
            link(nc.gpsimd.affine_select(out=band_sb[:, :], in_=band_sb[:, :], compare_op=ALU.is_ge, fill=OUTSIDE,
                                         base=WINDOW, pattern=[[-1, P]], channel_multiplier=1))
            link(nc.gpsimd.affine_select(out=band_sb[:, :], in_=band_sb[:, :], compare_op=ALU.is_ge, fill=OUTSIDE,
                                         base=WINDOW, pattern=[[1, P]], channel_multiplier=-1))
            nc.gpsimd.tensor_copy(identb_sb[:, :], ident_sb[:, :]).then_inc(consts_made, 1)

            def rstd1(p, s):
                pool.wait_ge(stats1_done, p * NB + NB)
                nc.gpsimd.tensor_scalar(var1_sb[:, s, :], mv1_sb[:, s, :, 1], 1.0, EPS,
                                        ALU.mult, ALU.add).then_inc(var1_done, 1)
                pool.wait_ge(var1_done, p + 1)
                nc.gpsimd.tensor_tensor(rstd1_sb[:, s, :], var1_sb[:, s, :], half_sb[:, :],
                                        ALU.pow).then_inc(rstd1_done, 1)

            def norm2(p, s):
                pool.wait_ge(stats2_done, p * NB + NB)
                nc.gpsimd.tensor_scalar(var2_sb[:, s, :], mv2_sb[:, s, :, 1], 1.0, EPS,
                                        ALU.mult, ALU.add).then_inc(var2_done, 1)
                nc.gpsimd.tensor_scalar(negmean2_sb[:, s, :], mv2_sb[:, s, :, 0], -1.0, 0.0,
                                        ALU.mult, ALU.add).then_inc(var2_done, 1)
                pool.wait_ge(var2_done, p * 2 + 2)
                nc.gpsimd.tensor_tensor(rstd2_sb[:, s, :], var2_sb[:, s, :], half_sb[:, :],
                                        ALU.pow).then_inc(rstd2_done, 1)
                pool.wait_ge(rstd2_done, p + 1)
                for h in range(NB):
                    nc.gpsimd.tensor_scalar(normed_sb[:, s, h].rearrange("p c r -> p (c r)"), x_sb[:, cols(p, h * D, D)],
                                            negmean2_sb[:, s, h:h + 1], rstd2_sb[:, s, h:h + 1],
                                            ALU.add, ALU.mult).then_inc(normed, 1)

            def step(i, parity, full=False):
                if full or i + 1 < PAIRS:
                    rstd1(i + 1, 1 - parity)
                if full or i >= 1:
                    norm2(i - 1, 1 - parity)

            rstd1(0, 0)
            run(pool, step, 0, LAST, 1, 7)
            for h in range(NB):
                pool.wait_ge(var2_last, h + 1)
                nc.gpsimd.tensor_tensor(rstd2_sb[:, LAST % 2, h:h + 1], var2_sb[:, LAST % 2, h:h + 1], half_sb[:, 0:1],
                                        ALU.pow).then_inc(rstd2_done, 1)

        @block.scalar
        def _(act):
            nc.scalar.preload_act_table(ACT.Exp)
            act.wait_ge(small_landed, 16)
            nc.scalar.activation(tanh_sb[:, :], scal_sb[:, 0:2], ACT.Tanh).then_inc(tanh_made, 1)

            def copy_keys(p, s):
                act.wait_ge(keys_done, p + 1)
                for c in range(DC):
                    ins = nc.scalar.activation(keys_sb[:, s, c].rearrange("p b k -> p (b k)"), keys_ps[:, c, :],
                                               ACT.Identity, bias=bc_sb[:, c:c + 1])
                ins.then_inc(keys_copied, 1)

            def softmax(p, s):
                for h in range(NB):
                    act.wait_ge(masked, p * NB + h + 1)
                    nc.scalar.activation(probs_sb[:, s, h], neg_sb[:, s, h], ACT.Exp, bias=negmin_sb[:, s, h:h + 1],
                                         scale=-1.0, accum_out=rowsum_sb[:, s, h:h + 1]).then_inc(probs_done, 1)

            def copy_probst(p, s):
                act.wait_ge(probst_done, p + 1)
                nc.scalar.copy(probst_sb[:, s], probst_ps[:, 0:NB, :]).then_inc(probst_copied, 1)

            def quantize(p, s):
                act.wait_ge(normedt_done, p + 1)
                if p is 0:
                    act.wait_ge(scales_made, 2)
                nc.scalar.activation(quant_sb[:, s].rearrange("p b c r -> p (b c r)"),
                                     normedt_ps[:, 0:NB].rearrange("p b c r -> p (b c r)"), ACT.Copy,
                                     scale=inv_sb[:, 0:1], saturate=False).then_inc(quantized, 1)

            def copy_y(p, s):
                act.wait_ge(ffn_done, p + 1)
                if p >= 2:
                    act.wait_ge(result_done, (p - 1) * NB)
                nc.scalar.activation(y_sb[:, s], ffn_ps[:, :, :], ACT.Copy, scale=prod_sb[:, 0:1]).then_inc(y_copied, 1)

            def quantize_last(h):
                act.wait_ge(normedt_done, LAST + h + 1)
                nc.scalar.activation(quant_sb[:, LAST % 2, h], normedt_at(LAST, h), ACT.Copy,
                                     scale=inv_sb[:, 0:1], saturate=False).then_inc(quantized, 1)

            def copy_y_last(h):
                act.wait_ge(ffn_done, LAST + h + 1)
                act.wait_ge(result_done, (LAST - 1) * NB)
                nc.scalar.activation(y_sb[:, LAST % 2, h], ffn_at(LAST, h), ACT.Copy,
                                     scale=prod_sb[:, 0:1]).then_inc(y_copied, 1)

            def step(i, parity, full=False):
                if full or i < PAIRS:
                    softmax(i, parity)
                if full or i >= 2:
                    quantize(i - 2, parity)
                if full or i < PAIRS:
                    copy_probst(i, parity)
                if full or i + 1 < PAIRS:
                    copy_keys(i + 1, 1 - parity)
                if full or i >= 2:
                    copy_y(i - 2, parity)

            act.wait_ge(b_centred, 1)
            copy_keys(0, 0)
            run(act, step, 0, PAIRS, 2, 6)
            for h in range(NB):
                quantize_last(h)
            for h in range(NB):
                copy_y_last(h)

        @block.vector
        def _(dve):
            made = [0]

            def link(ins):
                made[0] += 1
                ins.then_inc(dve_step, 1)
                dve.wait_ge(dve_step, made[0])

            def centre_weights():
                dve.wait_ge(w_landed, 16)
                for c in range(DC):
                    ins = nc.vector.bn_stats(wstat_sb[:, c, :], w_sb[:, c, :])
                link(ins)
                for c in range(DC):
                    ins = nc.vector.bn_aggr(wmean_sb[:, c, :], wstat_sb[:, c, :])
                link(ins)
                for c in range(DC):
                    nc.vector.tensor_scalar(wc_sb[:, c, :], w_sb[:, c, :], wmean_sb[:, c, 0:1], -1.0,
                                            ALU.subtract, ALU.mult).then_inc(w_centred, 1)

            def centre_bias():
                dve.wait_ge(small_landed, 16)
                link(nc.vector.bn_stats(wstat_sb[:, DC, :], brow_sb))
                link(nc.vector.bn_aggr(wmean_sb[:, DC, :], wstat_sb[:, DC, :]))
                nc.vector.tensor_scalar(bc_sb[:, :], bcol_sb, wmean_sb[:, DC, 0:1], -1.0,
                                        ALU.subtract, ALU.mult).then_inc(b_centred, 1)

            def scales():
                nc.vector.tensor_scalar(prod_sb[:, :], scal_sb[:, 2:3], scal_sb[:, 3:4], None,
                                        ALU.mult).then_inc(scales_made, 1)
                nc.vector.reciprocal(inv_sb[:, :], scal_sb[:, 2:4]).then_inc(scales_made, 1)

            def round_weights():
                dve.wait_ge(ffn_landed, 16)
                dve.wait_ge(scales_made, 2)
                link(nc.vector.tensor_scalar(r_u[:, :], wf_sb, inv_sb[:, 1:2], None, ALU.mult))
                link(nc.vector.tensor_scalar(r_m[:, :].bitcast(I32), r_u[:, :].bitcast(I32), 0x7F800000, None,
                                             ALU.bitwise_and))
                link(nc.vector.tensor_scalar(r_m[:, :], r_m[:, :], E4M3_LEAST_NORMAL, ROUND_4_BITS, ALU.max, ALU.mult))
                link(nc.vector.tensor_tensor(r_u[:, :], r_u[:, :], r_m[:, :], ALU.add))
                link(nc.vector.tensor_tensor(r_q[:, :], r_u[:, :], r_m[:, :], ALU.subtract))

            def spoil_overflows():
                link(nc.vector.tensor_scalar(r_c[:, :], r_q[:, :], E4M3_LARGEST, -E4M3_LARGEST, ALU.min, ALU.max))
                link(nc.vector.tensor_tensor(r_c[:, :], r_q[:, :], r_c[:, :], ALU.subtract))
                link(nc.vector.tensor_scalar(r_c[:, :], r_c[:, :], 3e38, 0.0, ALU.mult, ALU.mult))
                nc.vector.tensor_tensor(wq_sb[:, :, :].rearrange("p c f -> p (c f)"), r_q[:, :], r_c[:, :],
                                        ALU.add).then_inc(wq_made, 1)

            def bn1(p, s, h):
                if h == 0:
                    dve.wait_ge(x_landed[s], landed_count(p, s))
                nc.vector.bn_stats(bn1_sb[:, s, h, :], x_sb[:, cols(p, h * D, D)]).then_inc(bn1_done, 1)

            def aggr1(p, s):
                dve.wait_ge(bn1_done, p * NB + NB)
                for h in range(NB):
                    nc.vector.bn_aggr(mv1_sb[:, s, h, :], bn1_sb[:, s, h, :]).then_inc(stats1_done, 1)

            def mask(p, s):
                dve.wait_ge(rstd1_done, p + 1)
                for h in range(NB):
                    dve.wait_ge(scores_done, p * NB + h + 1)
                    nc.vector.tensor_tensor_reduce(neg_sb[:, s, h], scores_ps[h][:, 0:P], band_sb[:, :],
                                                   rstd1_sb[:, s, h:h + 1], 3e38, ALU.add, ALU.min,
                                                   negmin_sb[:, s, h:h + 1]).then_inc(masked, 1)

            def residual(p, s):
                dve.wait_ge(gate_done, p + 1)
                for h in range(NB):
                    dve.wait_ge(attn_done, p * NB + h + 1)
                    xs = x_sb[:, cols(p, h * D, D)]
                    nc.vector.scalar_tensor_tensor(out=xs, in0=attn_ps[h][:, 0:D], scalar=gate_sb[:, s, h:h + 1], in1=xs,
                                                   op0=ALU.mult, op1=ALU.add).then_inc(resid_done, 1)

            def bn2(p, s, h):
                dve.wait_ge(resid_done, p * NB + h + 1)
                nc.vector.bn_stats(bn2_sb[:, s, h, :], x_sb[:, cols(p, h * D, D)]).then_inc(bn2_done, 1)

            def aggr2(p, s):
                dve.wait_ge(bn2_done, p * NB + NB)
                for h in range(NB):
                    nc.vector.bn_aggr(mv2_sb[:, s, h, :], bn2_sb[:, s, h, :]).then_inc(stats2_done, 1)

            def reciprocal(p, s):
                dve.wait_ge(probs_done, p * NB + NB)
                nc.vector.reciprocal(recip_sb[:, s, :], rowsum_sb[:, s, :]).then_inc(recip_done, 1)

            def gate(p, s):
                dve.wait_ge(recip_done, p + 1)
                nc.vector.tensor_scalar(gate_sb[:, s, :], recip_sb[:, s, :], tanh_sb[:, 0:1], None,
                                        ALU.mult).then_inc(gate_done, 1)

            def add_bias(p, s):
                dve.wait_ge(y_copied, p + 1)
                nc.vector.tensor_tensor(y_sb[:, s], y_sb[:, s], bias_sb, ALU.add).then_inc(y_biased, 1)

            def result(p, s, h):
                dve.wait_ge(y_biased, p + 1 + (h if p is LAST else 0))
                xs = x_sb[:, cols(p, h * D, D)]
                nc.vector.scalar_tensor_tensor(out=xs, in0=y_sb[:, s, h], scalar=tanh_sb[:, 1:2], in1=xs,
                                               op0=ALU.mult, op1=ALU.add).then_inc(result_done, 1)

            def step(i, parity, full=False):
                other = 1 - parity
                if full or i >= 1:
                    residual(i - 1, other)
                if full or i < PAIRS:
                    mask(i, parity)
                if full or i + 1 < PAIRS:
                    bn1(i + 1, other, 0)
                    bn1(i + 1, other, 1)
                if full or i >= 1:
                    bn2(i - 1, other, 0)
                if full or i + 1 < PAIRS:
                    aggr1(i + 1, other)
                if full or i >= 1:
                    bn2(i - 1, other, 1)
                if full or i < PAIRS:
                    reciprocal(i, parity)
                if full or i >= 1:
                    aggr2(i - 1, other)
                if full or i >= 3:
                    add_bias(i - 3, other)
                if full or i < PAIRS:
                    gate(i, parity)
                if full or i >= 3:
                    for h in range(NB):
                        result(i - 3, other, h)
                if i is 0:
                    round_weights()
                if i is 1:
                    spoil_overflows()

            def variance_last(h):
                s = LAST % 2
                dve.wait_ge(bn2_done, LAST * NB + h + 1)
                nc.vector.bn_aggr(mv2_sb[:, s, h, :], bn2_sb[:, s, h, :]).then_inc(stats2_done, 1)
                dve.wait_ge(stats2_done, LAST * NB + h + 1)
                nc.vector.tensor_scalar(var2_sb[:, s, h:h + 1], mv2_sb[:, s, h, 1:2], EPS, None,
                                        ALU.add).then_inc(var2_last, 1)

            def norm_last(h):
                s = LAST % 2
                dve.wait_ge(rstd2_done, LAST + h + 1)
                nc.vector.tensor_scalar(normed_sb[:, s, h].rearrange("p c r -> p (c r)"), x_sb[:, cols(LAST, h * D, D)],
                                        mv2_sb[:, s, h, 0:1], rstd2_sb[:, s, h:h + 1],
                                        ALU.subtract, ALU.mult).then_inc(normed, 1)

            def finish(p):
                add_bias(p, p % 2)
                for h in range(NB):
                    result(p, p % 2, h)

            def finish_last(h):
                s = LAST % 2
                dve.wait_ge(y_copied, LAST + h + 1)
                nc.vector.tensor_tensor(y_sb[:, s, h], y_sb[:, s, h], bias_sb[:, h], ALU.add).then_inc(y_biased, 1)
                result(LAST, s, h)

            nc.vector.memset(warm_sb[:, :].bitcast(F32), 0.0).then_inc(zeros_made, 1)
            centre_weights()
            centre_bias()
            scales()
            bn1(0, 0, 0)
            bn1(0, 0, 1)
            aggr1(0, 0)
            dve.wait_ge(tanh_made, 1)
            dve.wait_ge(consts_made, 1)
            run(dve, step, 0, LAST, 3, 7)
            residual(LAST, LAST % 2)
            for h in range(NB):
                bn2(LAST, LAST % 2, h)
                variance_last(h)
            finish(LAST - 2)
            for h in range(NB):
                norm_last(h)
            finish(LAST - 1)
            for h in range(NB):
                finish_last(h)

        @block.tensor
        def _(pe):
            def keys(p, s, o):
                if o == 0:
                    pe.wait_ge(ctxt_landed[s], landed_count(p, s))
                    if p is not 0:
                        pe.wait_ge(keys_copied, p)
                for c in range(DC):
                    if p is 0 and o == 0:
                        pe.wait_ge(w_centred, c + 1)
                    ins = nc.tensor.matmul(keys_ps[:, o, :], wc_sb[:, c, o * P:(o + 1) * P],
                                           ctxt_sb[:, cols(p, c * NB * P, NB * P)],
                                           start=(c == 0), stop=(c == DC - 1))
                if o == DC - 1:
                    ins.then_inc(keys_done, 1)

            def scores(p, s):
                pe.wait_ge(xt_landed[s], landed_count(p, s))
                pe.wait_ge(keys_copied, p + 1)
                if p is not 0:
                    pe.wait_ge(masked, p * NB)
                for h in range(NB):
                    for c in range(DC):
                        ins = nc.tensor.matmul(scores_ps[h][:, 0:P], xt_sb[:, s, c, h, :], keys_sb[:, s, c, h, :],
                                               start=(c == 0), stop=(c == DC - 1))
                    ins.then_inc(scores_done, 1)

            def transpose_probs(p, s):
                pe.wait_ge(probs_done, p * NB + NB)
                if p is not 0:
                    pe.wait_ge(probst_copied, p)
                for h in range(NB):
                    ins = nc.tensor.transpose(probst_ps[:, h, :], probs_sb[:, s, h], ident_sb[:, :])
                ins.then_inc(probst_done, 1)

            def attend(p, s):
                pe.wait_ge(ctx_landed[s], landed_count(p, s))
                pe.wait_ge(probst_copied, p + 1)
                if p is not 0:
                    pe.wait_ge(resid_done, p * NB)
                for h in range(NB):
                    nc.tensor.matmul(attn_ps[h][:, 0:D], probst_sb[:, s, h], ctx_sb[:, cols(p, h * D, D)],
                                     start=True, stop=True).then_inc(attn_done, 1)

            def transpose_normed(p, s, batches):
                pe.wait_ge(normed, p * NB + batches[-1] + 1)
                if p is LAST and batches[0] == 1:
                    pe.wait_ge(masked, PAIRS * NB)
                elif p is not 0:
                    pe.wait_ge(quantized, p)
                for h in batches:
                    for c in range(DC):
                        ins = nc.tensor.transpose(normedt_at(p, h)[:, c, :], normed_sb[:, s, h, c, :], identb_sb[:, :])
                ins.then_inc(normedt_done, 1)

            def ffn(p, s, batches):
                pe.wait_ge(quantized, p + 1 + (batches[0] if p is LAST else 0))
                if p is 0:
                    pe.wait_ge(wq_made, 1)
                elif p is LAST and batches[0] == 1:
                    pe.wait_ge(masked, PAIRS * NB)
                else:
                    pe.wait_ge(y_copied, p)
                for h in batches:
                    for c in range(DC):
                        ins = nc.tensor.matmul(ffn_at(p, h), quant_sb[:, s, h, c, :], wq_sb[:, c, :],
                                               start=(c == 0), stop=(c == DC - 1))
                ins.then_inc(ffn_done, 1)

            def step(i, parity, full=False):
                if full or i < PAIRS:
                    scores(i, parity)
                if full or i + 1 < PAIRS:
                    keys(i + 1, 1 - parity, 0)
                if full or i >= 2:
                    transpose_normed(i - 2, parity, range(NB))
                if full or i < PAIRS:
                    transpose_probs(i, parity)
                if full or i + 1 < PAIRS:
                    keys(i + 1, 1 - parity, 1)
                if full or i >= 2:
                    ffn(i - 2, parity, range(NB))
                if full or i < PAIRS:
                    attend(i, parity)

            pe.wait_ge(zeros_made, 1)
            for _ in range(WARM_UP):
                nc.tensor.matmul(attn_ps[0][:, 0:PAIR], warm_sb[:, 0:P], warm_sb[:, :], start=True, stop=True)
            for o in range(DC):
                keys(0, 0, o)
            pe.wait_ge(consts_made, 1)
            run(pe, step, 0, PAIRS, 2, 6)
            for h in range(NB):
                transpose_normed(LAST, LAST % 2, [h])
            for h in range(NB):
                ffn(LAST, LAST % 2, [h])


def kernel(x, ctx_1024, g_xattn, g_ffn, L0_xattn_W_reduce, L0_xattn_b_reduce, L0_ffn_kernel, L0_ffn_input_scale,
           L0_ffn_kernel_scale, L0_ffn_bias):
    import numpy as np
    import concourse.bacc as bacc
    from concourse.bass_utils import run_bass_kernel_spmd

    x, ctx, w, wf = (np.asarray(a) for a in (x, ctx_1024, L0_xattn_W_reduce, L0_ffn_kernel))
    B, S, D = x.shape
    chunks = D // P

    def rows(a):
        return np.ascontiguousarray(a.transpose(1, 0, 2).reshape(S, B * D))

    def features(a):
        return np.ascontiguousarray(a.reshape(B // 2, 2, S, chunks, P).transpose(4, 0, 3, 1, 2).reshape(P, B * D))

    def across(a):
        return np.broadcast_to(np.asarray(a), (P, a.shape[0]))

    arrays = {
        "x": rows(x),
        "x_t": features(x),
        "ctx": rows(ctx),
        "ctx_t": features(ctx),
        "w_t": np.ascontiguousarray(w.T.reshape(chunks, P, D).transpose(1, 0, 2).reshape(P, chunks * D)),
        "small": np.concatenate([*(across(a) for a in (g_xattn, g_ffn, L0_ffn_input_scale, L0_ffn_kernel_scale)),
                                 np.asarray(L0_xattn_b_reduce).reshape(chunks, P).T, across(L0_xattn_b_reduce)], axis=1),
        "ffn_consts": np.concatenate([wf.reshape(chunks, P, D).transpose(1, 0, 2).reshape(P, chunks * D),
                                      across(L0_ffn_bias), across(L0_ffn_bias)], axis=1),
    }
    nc = bacc.Bacc("TRN2", target_bir_lowering=False, num_devices=1)
    args = [nc.dram_tensor(f"in_{name}", a.shape, mybir.dt.from_np(a.dtype), kind="ExternalInput").ap()
            for name, a in arrays.items()]
    out = nc.dram_tensor("out", (S, B * D), F32, kind="ExternalOutput").ap()
    flamingo_block(nc, *args, out)
    r = run_bass_kernel_spmd(nc, [{f"in_{name}": a for name, a in arrays.items()}], core_ids=[0])
    got = r.results[0]["out"]
    return np.ascontiguousarray(got.reshape(S, B, D).transpose(1, 0, 2))
```

```python
from contextlib import ExitStack

import concourse.bass as bass
from concourse import mybir

F32 = mybir.dt.float32
BF16 = mybir.dt.bfloat16
FP8 = mybir.dt.float8e4
I32 = mybir.dt.int32
ALU = mybir.AluOpType
ACT = mybir.ActivationFunctionType

P = 128
WINDOW = 20
EPS = 1e-5
OUTSIDE = 1e30
ROUND_4_BITS = 1.5 * 2.0 ** 20
E4M3_LEAST_NORMAL = 2.0 ** -6
E4M3_LARGEST_FINITE = 3.4e38 / 464
CHIP_E4M3_LARGEST = 240.0
WARM_UP = 8


def flamingo_block(nc, x, x_t, ctx, ctx_t, w_t, small, ffn_consts, out):
    D = 256
    DC = D // P
    PAIR = 2 * D
    PAIRS = x.shape[1] // PAIR
    NB = 2
    LAST = PAIRS - 1
    Y_THIRD = 2
    ASIDE = LAST - 2
    assert x.shape[0] == P and PAIRS >= 8 and PAIRS % 2 == 0

    with ExitStack() as stack:
        def sb(name, shape, dt=F32):
            return stack.enter_context(nc.sbuf_tensor(name, shape, dt))

        def bank(name, shape, dt=F32):
            return stack.enter_context(nc.psum_tensor(name, shape, dt))

        def sem(name):
            return stack.enter_context(nc.semaphore(name))

        x_sb = sb("x_sb", [P, PAIRS * PAIR])
        ctx_sb = sb("ctx_sb", [P, PAIRS * PAIR])
        ctxt_sb = sb("ctxt_sb", [P, PAIRS * PAIR])
        xt_sb = sb("xt_sb", [P, 2, DC, NB, P])
        keys_sb = sb("keys_sb", [P, 2, DC, NB, P])
        neg_sb = sb("neg_sb", [P, 2, NB, P])
        probs_sb = sb("probs_sb", [P, 2, NB, P])
        probst_sb = sb("probst_sb", [P, 2, NB, P])
        normed_sb = sb("normed_sb", [P, 2, NB, DC, P], BF16)
        quant_sb = sb("quant_sb", [P, 2, NB, DC, P], FP8)
        scaled_sb = sb("scaled_sb", [P, NB, DC * P])
        wide_sb = sb("wide_sb", [P, 2, NB, DC, P], BF16)
        y_sb = sb("y_sb", [P, 3, NB, D], BF16)
        gated_sb = sb("gated_sb", [P, NB * D])
        negmin_sb = sb("negmin_sb", [P, 2, NB])
        rowsum_sb = sb("rowsum_sb", [P, 2, NB])
        recip_sb = sb("recip_sb", [P, 2, NB])
        bn1_sb = sb("bn1_sb", [P, 2, NB, 6])
        mv1_sb = sb("mv1_sb", [P, 2, NB, 2])
        var1_sb = sb("var1_sb", [P, 2, NB])
        rstd1_sb = sb("rstd1_sb", [P, 2, NB])
        bn2_sb = sb("bn2_sb", [P, 2, NB, 6])
        mv2_sb = sb("mv2_sb", [P, 2, NB, 2])
        var2_sb = sb("var2_sb", [P, 2, NB])
        negmean2_sb = sb("negmean2_sb", [P, 2, NB])
        rstd2_sb = sb("rstd2_sb", [P, 2, NB])
        w_sb = sb("w_sb", [P, DC, D])
        wc_sb = sb("wc_sb", [P, DC, D])
        wstat_sb = sb("wstat_sb", [P, DC + 1, 6])
        wmean_sb = sb("wmean_sb", [P, DC + 1, 2])
        small_sb = sb("small_sb", [P, 4 + DC + D])
        scal_sb = small_sb[:, 0:4]
        bcol_sb = small_sb[:, 4:4 + DC]
        brow_sb = small_sb[:, 4 + DC:4 + DC + D]
        bc_sb = sb("bc_sb", [P, DC])
        ffnc_sb = sb("ffnc_sb", [P, (DC + NB) * D], BF16)
        wf_sb = ffnc_sb[:, 0:DC * D]
        bias_sb = ffnc_sb[:, DC * D:(DC + NB) * D].rearrange("p (b f) -> p b f", b=NB)
        wq_sb = sb("wq_sb", [P, DC, D], BF16)
        tanh_sb = sb("tanh_sb", [P, 2])
        inv_sb = sb("inv_sb", [P, 2])
        prod_sb = sb("prod_sb", [P, 1])
        half_sb = sb("half_sb", [P, NB])
        band_sb = sb("band_sb", [P, P])
        ident_sb = sb("ident_sb", [P, P])
        identb_sb = sb("identb_sb", [P, P], BF16)
        is_wide_sb = sb("is_wide_sb", [P, 1], I32)
        wscaled_sb = sb("wscaled_sb", [P, DC * D])
        magic_sb = sb("magic_sb", [P, DC * D])
        rounded_sb = sb("rounded_sb", [P, DC * D], BF16)
        spoil_sb = sb("spoil_sb", [P, DC * D], BF16)
        warm_sb = sb("warm_sb", [P, PAIR], BF16)

        keys_ps = bank("keys_ps", [P, DC, NB * P])
        scores_ps = [bank(f"scores_ps{h}", [P, 512]) for h in range(NB)]
        probst_ps = bank("probst_ps", [P, 4, P])
        attn_ps = [bank(f"attn_ps{h}", [P, 512]) for h in range(NB)]
        normedt_ps = bank("normedt_ps", [P, 2 * NB, DC, P], BF16)
        ffn_ps = bank("ffn_ps", [P, NB, D])

        def as_transposed(bank):
            return bank.bitcast(BF16).rearrange("p (c r) -> p c r", c=DC)

        def normedt_at(p, h):
            if p >= LAST - 1 and h == 1:
                return as_transposed(keys_ps[:, 1, 0:P] if p == LAST - 1 else scores_ps[1][:, 0:P])
            return normedt_ps[:, h]

        def transposed_count(p, h):
            return p + 1 if p < LAST - 1 else LAST + NB * (p - LAST + 1) + h

        def probst_at(h):
            return probst_ps[:, 0, :] if h == 0 else keys_ps[:, 0, 0:P]

        def keys_at(p, o):
            return ffn_ps[:, 0] if p == 0 and o == 1 else keys_ps[:, o, :]

        def ffn_at(p, h):
            return (attn_ps[0], scores_ps[0])[h][:, 0:D] if p == LAST else ffn_ps[:, h, :]

        x_landed = [sem("x_landed0"), sem("x_landed1")]
        xt_landed = [sem("xt_landed0"), sem("xt_landed1")]
        ctx_landed = [sem("ctx_landed0"), sem("ctx_landed1")]
        ctxt_landed = [sem("ctxt_landed0"), sem("ctxt_landed1")]
        w_landed = [sem("w_landed0"), sem("w_landed1")]
        small_landed = sem("small_landed")
        ffn_landed = sem("ffn_landed")
        stored = sem("stored")
        pool_step = sem("pool_step")
        consts_made = sem("consts_made")
        tanh_made = sem("tanh_made")
        scales_made = sem("scales_made")
        wstats_done = sem("wstats_done")
        wmeans_done = sem("wmeans_done")
        w_centred = sem("w_centred")
        b_centred = sem("b_centred")
        zeros_made = sem("zeros_made")
        wide_decided = sem("wide_decided")
        magic_made = sem("magic_made")
        weights_rounded = sem("weights_rounded")
        dve_step = sem("dve_step")
        wq_made = sem("wq_made")
        keys_done = sem("keys_done")
        first_keys_copied = sem("first_keys_copied")
        keys_copied = sem("keys_copied")
        scores_done = sem("scores_done")
        masked = sem("masked")
        probs_done = sem("probs_done")
        probst_done = sem("probst_done")
        probst_copied = sem("probst_copied")
        attn_done = sem("attn_done")
        recip_done = sem("recip_done")
        resid_done = sem("resid_done")
        bn1_done = sem("bn1_done")
        stats1_done = sem("stats1_done")
        var1_done = sem("var1_done")
        rstd1_done = sem("rstd1_done")
        bn2_done = sem("bn2_done")
        stats2_done = sem("stats2_done")
        var2_done = sem("var2_done")
        rstd2_done = sem("rstd2_done")
        var2_last = sem("var2_last")
        normed = sem("normed")
        normedt_done = sem("normedt_done")
        quantized = sem("quantized")
        scaled_done = sem("scaled_done")
        ffn_done = sem("ffn_done")
        y_copied = sem("y_copied")
        y_biased = sem("y_biased")
        result_done = sem("result_done")
        aside_done = sem("aside_done")

        block = stack.enter_context(nc.Block())

        def landed_count(p, parity):
            return (p - parity) * 8 + 16

        def take_magic(link, u, magic):
            link(nc.vector.tensor_scalar(magic.bitcast(I32), u.bitcast(I32), 0x7F800000, None, ALU.bitwise_and))
            return nc.vector.tensor_scalar(magic, magic, E4M3_LEAST_NORMAL, ROUND_4_BITS, ALU.max, ALU.mult)

        def spoil_overflows(link, rounded, zeros_or_nan, out_e4m3):
            link(nc.vector.tensor_scalar(zeros_or_nan, rounded, E4M3_LARGEST_FINITE, 0.0, ALU.mult, ALU.mult))
            return nc.vector.tensor_tensor(out_e4m3, rounded, zeros_or_nan, ALU.add)

        def branch(engine, program):
            engine.wait_ge(wide_decided, 1)
            is_wide = engine.value_load(is_wide_sb[0:1, 0:1], min_val=0, max_val=1)
            with engine.If(is_wide == 0):
                program(False)
            with engine.Else():
                program(True)

        def cols(p, start, size):
            return bass.ds(p * PAIR + start, size)

        @block.sync
        def _(sp):
            def load(p, parity, first=False):
                for dst, src, landed in ((ctxt_sb, ctx_t, ctxt_landed), (x_sb, x, x_landed), (ctx_sb, ctx, ctx_landed)):
                    if not first:
                        sp.wait_ge(landed[parity], landed_count(p - 2, parity))
                    sp.dma_start(dst[:, cols(p, 0, PAIR)], src[:, cols(p, 0, PAIR)]).then_inc(landed[parity], 16)
                    if dst is x_sb and first and p == 0:
                        sp.dma_start(ffnc_sb[:, :], ffn_consts).then_inc(ffn_landed, 16)
                    if dst is ctxt_sb:
                        if first and p == 0:
                            sp.dma_start(small_sb[:, :], small).then_inc(small_landed, 16)
                        if not first:
                            sp.wait_ge(scores_done, (p - 2) * NB + NB)
                        sp.dma_start(xt_sb[:, parity].rearrange("p c b r -> p (c b r)"),
                                     x_t[:, cols(p, 0, PAIR)]).then_inc(xt_landed[parity], 16)

            def store(p):
                if p == ASIDE:
                    sp.wait_ge(aside_done, 2)
                else:
                    sp.wait_ge(result_done, p * NB + (NB if p < ASIDE else 0))
                sp.dma_start(out[:, cols(p, 0, PAIR)], x_sb[:, cols(p, 0, PAIR)]).then_inc(stored, 16)

            def store_last(h):
                sp.wait_ge(result_done, (LAST - 1) * NB + h + 1)
                sp.dma_start(out[:, cols(LAST, h * D, D)], x_sb[:, cols(LAST, h * D, D)]).then_inc(stored, 16)

            def step(i, parity):
                if i + 2 < PAIRS:
                    load(i + 2, parity)
                if i >= 3:
                    store(i - 3)

            for c in range(DC):
                sp.dma_start(w_sb[:, c, :], w_t[:, c * D:(c + 1) * D]).then_inc(w_landed[c], 16)
            load(0, 0, first=True)
            load(1, 1, first=True)
            for i in range(PAIRS):
                step(i, i % 2)
            store(LAST - 1)
            store(ASIDE)
            for h in range(NB):
                store_last(h)
            sp.wait_ge(stored, 16 * (LAST + NB))

        @block.gpsimd
        def _(pool):
            made = [0]

            def link(ins):
                made[0] += 1
                ins.then_inc(pool_step, 1)
                pool.wait_ge(pool_step, made[0])

            link(nc.gpsimd.memset(ident_sb[:, :], 0.0))
            link(nc.gpsimd.affine_select(out=ident_sb[:, :], in_=ident_sb[:, :], compare_op=ALU.not_equal, fill=1.0,
                                         base=0, pattern=[[-1, P]], channel_multiplier=1))
            link(nc.gpsimd.memset(half_sb[:, :], -0.5))
            link(nc.gpsimd.memset(band_sb[:, :], 0.0))
            link(nc.gpsimd.affine_select(out=band_sb[:, :], in_=band_sb[:, :], compare_op=ALU.is_ge, fill=OUTSIDE,
                                         base=WINDOW, pattern=[[-1, P]], channel_multiplier=1))
            link(nc.gpsimd.affine_select(out=band_sb[:, :], in_=band_sb[:, :], compare_op=ALU.is_ge, fill=OUTSIDE,
                                         base=WINDOW, pattern=[[1, P]], channel_multiplier=-1))
            nc.gpsimd.tensor_copy(identb_sb[:, :], ident_sb[:, :]).then_inc(consts_made, 1)

            def rstd1(p, s):
                pool.wait_ge(stats1_done, p * NB + NB)
                nc.gpsimd.tensor_scalar(var1_sb[:, s, :], mv1_sb[:, s, :, 1], 1.0, EPS,
                                        ALU.mult, ALU.add).then_inc(var1_done, 1)
                pool.wait_ge(var1_done, p + 1)
                nc.gpsimd.tensor_tensor(rstd1_sb[:, s, :], var1_sb[:, s, :], half_sb[:, :],
                                        ALU.pow).then_inc(rstd1_done, 1)

            def norm2(p, s):
                pool.wait_ge(stats2_done, p * NB + NB)
                nc.gpsimd.tensor_scalar(var2_sb[:, s, :], mv2_sb[:, s, :, 1], 1.0, EPS,
                                        ALU.mult, ALU.add).then_inc(var2_done, 1)
                nc.gpsimd.tensor_scalar(negmean2_sb[:, s, :], mv2_sb[:, s, :, 0], -1.0, 0.0,
                                        ALU.mult, ALU.add).then_inc(var2_done, 1)
                pool.wait_ge(var2_done, p * 2 + 2)
                nc.gpsimd.tensor_tensor(rstd2_sb[:, s, :], var2_sb[:, s, :], half_sb[:, :],
                                        ALU.pow).then_inc(rstd2_done, 1)
                pool.wait_ge(rstd2_done, p + 1)
                for h in range(NB):
                    nc.gpsimd.tensor_scalar(normed_sb[:, s, h].rearrange("p c r -> p (c r)"), x_sb[:, cols(p, h * D, D)],
                                            negmean2_sb[:, s, h:h + 1], rstd2_sb[:, s, h:h + 1],
                                            ALU.add, ALU.mult).then_inc(normed, 1)

            def step(i, parity):
                if i + 1 < PAIRS:
                    rstd1(i + 1, 1 - parity)
                if i >= 1:
                    norm2(i - 1, 1 - parity)

            pool.wait_ge(small_landed, 16)
            nc.gpsimd.tensor_scalar(is_wide_sb[:, :], scal_sb[:, 2:3], scal_sb[:, 2:3], D / CHIP_E4M3_LARGEST ** 2,
                                    ALU.mult, ALU.is_lt).then_inc(wide_decided, 1)

            def round_weights():
                pool.wait_ge(magic_made, 1)
                nc.gpsimd.tensor_tensor(wscaled_sb[:, :], wscaled_sb[:, :], magic_sb[:, :],
                                        ALU.add).then_inc(weights_rounded, 1)
                pool.wait_ge(weights_rounded, 1)
                nc.gpsimd.tensor_tensor(rounded_sb[:, :], wscaled_sb[:, :], magic_sb[:, :],
                                        ALU.subtract).then_inc(weights_rounded, 1)

            rstd1(0, 0)
            round_weights()
            for i in range(PAIRS):
                step(i, i % 2)
            for h in range(NB):
                pool.wait_ge(var2_last, h + 1)
                nc.gpsimd.tensor_tensor(rstd2_sb[:, LAST % 2, h:h + 1], var2_sb[:, LAST % 2, h:h + 1], half_sb[:, 0:1],
                                        ALU.pow).then_inc(rstd2_done, 1)
            pool.wait_ge(y_biased, ASIDE + 1)
            nc.gpsimd.tensor_scalar(gated_sb[:, :], y_sb[:, ASIDE % 2].rearrange("p b f -> p (b f)"),
                                    tanh_sb[:, 1:2], 0.0, ALU.mult, ALU.add).then_inc(aside_done, 1)
            pool.wait_ge(aside_done, 1)
            xs = x_sb[:, cols(ASIDE, 0, PAIR)]
            nc.gpsimd.tensor_tensor(xs, xs, gated_sb[:, :], ALU.add).then_inc(aside_done, 1)

        @block.scalar
        def _(act):
            nc.scalar.preload_act_table(ACT.Exp)
            act.wait_ge(small_landed, 16)
            nc.scalar.activation(tanh_sb[:, :], scal_sb[:, 0:2], ACT.Tanh).then_inc(tanh_made, 1)

            def copy_keys(p, s):
                for c in range(DC):
                    act.wait_ge(keys_done, p + DC if p != 0 else c + 1)
                    ins = nc.scalar.activation(keys_sb[:, s, c].rearrange("p b k -> p (b k)"), keys_at(p, c),
                                               ACT.Identity, bias=bc_sb[:, c:c + 1])
                    if p == 0:
                        ins.then_inc(first_keys_copied, 1)
                if p > 0:
                    ins.then_inc(keys_copied, 1)

            def softmax(p, s):
                for h in range(NB):
                    act.wait_ge(masked, p * NB + h + 1)
                    nc.scalar.activation(probs_sb[:, s, h], neg_sb[:, s, h], ACT.Exp, bias=negmin_sb[:, s, h:h + 1],
                                         scale=-1.0, accum_out=rowsum_sb[:, s, h:h + 1]).then_inc(probs_done, 1)

            def copy_probst(p, s):
                act.wait_ge(probst_done, p + 1)
                if p == 0:
                    act.wait_ge(tanh_made, 1)
                nc.scalar.activation(probst_sb[:, s], probst_ps[:, 0:NB, :], ACT.Copy,
                                     scale=tanh_sb[:, 0:1]).then_inc(probst_copied, 1)

            def copy_probst_last(h):
                act.wait_ge(probst_done, LAST + h + 1)
                nc.scalar.activation(probst_sb[:, LAST % 2, h], probst_at(h), ACT.Copy,
                                     scale=tanh_sb[:, 0:1]).then_inc(probst_copied, 1)

            def scale_wide(p, h):
                nc.scalar.activation(scaled_sb[:, h], normedt_at(p, h).rearrange("p c r -> p (c r)"), ACT.Copy,
                                     scale=inv_sb[:, 0:1]).then_inc(scaled_done, 1)

            def quantize(p, s, wide):
                act.wait_ge(normedt_done, p + 1)
                if p == 0:
                    act.wait_ge(scales_made, 2)
                if wide:
                    for h in range(NB):
                        scale_wide(p, h)
                    return
                nc.scalar.activation(quant_sb[:, s].rearrange("p b c r -> p (b c r)"),
                                     normedt_ps[:, 0:NB].rearrange("p b c r -> p (b c r)"), ACT.Copy,
                                     scale=inv_sb[:, 0:1], saturate=False).then_inc(quantized, 1)

            def copy_y(p, s):
                act.wait_ge(ffn_done, p + 1)
                if p >= 2 and s != Y_THIRD:
                    act.wait_ge(result_done, (p - 1) * NB)
                nc.scalar.activation(y_sb[:, s], ffn_ps[:, :, :], ACT.Copy, scale=prod_sb[:, 0:1]).then_inc(y_copied, 1)

            def quantize_batch(p, h, wide):
                act.wait_ge(normedt_done, transposed_count(p, h))
                if wide:
                    scale_wide(p, h)
                    return
                nc.scalar.activation(quant_sb[:, p % 2, h], normedt_at(p, h), ACT.Copy,
                                     scale=inv_sb[:, 0:1], saturate=False).then_inc(quantized, 1)

            def copy_y_last(h):
                act.wait_ge(ffn_done, LAST + h + 1)
                act.wait_ge(aside_done, 1)
                nc.scalar.activation(y_sb[:, LAST % 2, h], ffn_at(LAST, h), ACT.Copy,
                                     scale=prod_sb[:, 0:1]).then_inc(y_copied, 1)

            def program(wide):
                def step(i, parity):
                    softmax(i, parity)
                    if i < LAST:
                        if i >= 2:
                            quantize(i - 2, parity, wide)
                        copy_probst(i, parity)
                        copy_keys(i + 1, 1 - parity)
                    else:
                        for h in range(NB):
                            copy_probst_last(h)
                        quantize(i - 2, parity, wide)
                    if i >= 2:
                        copy_y(i - 2, parity)

                act.wait_ge(b_centred, 1)
                copy_keys(0, 0)
                for i in range(PAIRS):
                    step(i, i % 2)
                for h in range(NB):
                    quantize_batch(LAST - 1, h, wide)
                copy_y(LAST - 1, Y_THIRD)
                for h in range(NB):
                    quantize_batch(LAST, h, wide)
                for h in range(NB):
                    copy_y_last(h)

            branch(act, program)

        @block.vector
        def _(dve):
            made = [0]

            def link(ins):
                made[0] += 1
                ins.then_inc(dve_step, 1)
                dve.wait_ge(dve_step, made[0])

            def centre_weights():
                for c in range(DC):
                    dve.wait_ge(w_landed[c], 16)
                    nc.vector.bn_stats(wstat_sb[:, c, :], w_sb[:, c, :]).then_inc(wstats_done, 1)
                for c in range(DC):
                    dve.wait_ge(wstats_done, c + 1)
                    nc.vector.bn_aggr(wmean_sb[:, c, :], wstat_sb[:, c, :]).then_inc(wmeans_done, 1)
                for o in range(DC):
                    for c in range(DC):
                        dve.wait_ge(wmeans_done, c + 1)
                        nc.vector.tensor_scalar(wc_sb[:, c, o * P:(o + 1) * P], w_sb[:, c, o * P:(o + 1) * P],
                                                wmean_sb[:, c, 0:1], -1.0,
                                                ALU.subtract, ALU.mult).then_inc(w_centred, 1)

            def centre_bias():
                dve.wait_ge(small_landed, 16)
                link(nc.vector.bn_stats(wstat_sb[:, DC, :], brow_sb))
                link(nc.vector.bn_aggr(wmean_sb[:, DC, :], wstat_sb[:, DC, :]))
                nc.vector.tensor_scalar(bc_sb[:, :], bcol_sb, wmean_sb[:, DC, 0:1], -1.0,
                                        ALU.subtract, ALU.mult).then_inc(b_centred, 1)

            def scales():
                nc.vector.tensor_scalar(prod_sb[:, :], scal_sb[:, 2:3], scal_sb[:, 3:4], None,
                                        ALU.mult).then_inc(scales_made, 1)
                nc.vector.reciprocal(inv_sb[:, :], scal_sb[:, 2:4]).then_inc(scales_made, 1)

            def scale_weights():
                dve.wait_ge(ffn_landed, 16)
                dve.wait_ge(scales_made, 2)
                link(nc.vector.tensor_scalar(wscaled_sb[:, :], wf_sb, inv_sb[:, 1:2], None, ALU.mult))
                take_magic(link, wscaled_sb[:, :], magic_sb[:, :]).then_inc(magic_made, 1)

            def finish_weights():
                dve.wait_ge(weights_rounded, 2)
                spoil_overflows(link, rounded_sb[:, :], spoil_sb[:, :],
                                wq_sb[:, :, :].rearrange("p c f -> p (c f)")).then_inc(wq_made, 1)

            def bn1(p, s, h):
                if h == 0:
                    dve.wait_ge(x_landed[s], landed_count(p, s))
                nc.vector.bn_stats(bn1_sb[:, s, h, :], x_sb[:, cols(p, h * D, D)]).then_inc(bn1_done, 1)

            def aggr1(p, s):
                dve.wait_ge(bn1_done, p * NB + NB)
                for h in range(NB):
                    nc.vector.bn_aggr(mv1_sb[:, s, h, :], bn1_sb[:, s, h, :]).then_inc(stats1_done, 1)

            def mask(p, s):
                dve.wait_ge(rstd1_done, p + 1)
                for h in range(NB):
                    dve.wait_ge(scores_done, p * NB + h + 1)
                    nc.vector.tensor_tensor_reduce(neg_sb[:, s, h], scores_ps[h][:, 0:P], band_sb[:, :],
                                                   rstd1_sb[:, s, h:h + 1], 3e38, ALU.add, ALU.min,
                                                   negmin_sb[:, s, h:h + 1]).then_inc(masked, 1)

            def residual(p, s):
                dve.wait_ge(recip_done, p + 1)
                for h in range(NB):
                    dve.wait_ge(attn_done, p * NB + h + 1)
                    xs = x_sb[:, cols(p, h * D, D)]
                    nc.vector.scalar_tensor_tensor(out=xs, in0=attn_ps[h][:, 0:D], scalar=recip_sb[:, s, h:h + 1], in1=xs,
                                                   op0=ALU.mult, op1=ALU.add).then_inc(resid_done, 1)

            def bn2(p, s, h):
                dve.wait_ge(resid_done, p * NB + h + 1)
                nc.vector.bn_stats(bn2_sb[:, s, h, :], x_sb[:, cols(p, h * D, D)]).then_inc(bn2_done, 1)

            def aggr2(p, s):
                dve.wait_ge(bn2_done, p * NB + NB)
                for h in range(NB):
                    nc.vector.bn_aggr(mv2_sb[:, s, h, :], bn2_sb[:, s, h, :]).then_inc(stats2_done, 1)

            def reciprocal(p, s):
                dve.wait_ge(probs_done, p * NB + NB)
                nc.vector.reciprocal(recip_sb[:, s, :], rowsum_sb[:, s, :]).then_inc(recip_done, 1)

            def add_bias(p, s):
                dve.wait_ge(y_copied, p + 1)
                nc.vector.tensor_tensor(y_sb[:, s], y_sb[:, s], bias_sb, ALU.add).then_inc(y_biased, 1)

            def result(p, s, h):
                dve.wait_ge(y_biased, p + 1 + (h if p == LAST else 0))
                xs = x_sb[:, cols(p, h * D, D)]
                nc.vector.scalar_tensor_tensor(out=xs, in0=y_sb[:, s, h], scalar=tanh_sb[:, 1:2], in1=xs,
                                               op0=ALU.mult, op1=ALU.add).then_inc(result_done, 1)

            def round_wide(p, s, h):
                dve.wait_ge(scaled_done, p * NB + h + 1)
                magic, rounded = magic_sb[:, 0:DC * P], rounded_sb[:, 0:DC * P]
                link(take_magic(link, scaled_sb[:, h], magic))
                link(nc.vector.tensor_tensor(scaled_sb[:, h], scaled_sb[:, h], magic, ALU.add))
                link(nc.vector.tensor_tensor(rounded, scaled_sb[:, h], magic, ALU.subtract))
                ins = spoil_overflows(link, rounded, spoil_sb[:, 0:DC * P],
                                      wide_sb[:, s, h].rearrange("p c r -> p (c r)"))
                if p >= LAST - 1 or h == NB - 1:
                    ins.then_inc(quantized, 1)

            def variance_last(h):
                s = LAST % 2
                dve.wait_ge(bn2_done, LAST * NB + h + 1)
                nc.vector.bn_aggr(mv2_sb[:, s, h, :], bn2_sb[:, s, h, :]).then_inc(stats2_done, 1)
                dve.wait_ge(stats2_done, LAST * NB + h + 1)
                nc.vector.tensor_scalar(var2_sb[:, s, h:h + 1], mv2_sb[:, s, h, 1:2], EPS, None,
                                        ALU.add).then_inc(var2_last, 1)

            def norm_last(h):
                s = LAST % 2
                dve.wait_ge(rstd2_done, LAST + h + 1)
                nc.vector.tensor_scalar(normed_sb[:, s, h].rearrange("p c r -> p (c r)"), x_sb[:, cols(LAST, h * D, D)],
                                        mv2_sb[:, s, h, 0:1], rstd2_sb[:, s, h:h + 1],
                                        ALU.subtract, ALU.mult).then_inc(normed, 1)

            def finish_last(h):
                s = LAST % 2
                dve.wait_ge(y_copied, LAST + h + 1)
                nc.vector.tensor_tensor(y_sb[:, s, h], y_sb[:, s, h], bias_sb[:, h], ALU.add).then_inc(y_biased, 1)
                result(LAST, s, h)

            def program(wide):
                made[0] = steps_before

                def step(i, parity):
                    other = 1 - parity
                    if i >= 1:
                        residual(i - 1, other)
                    mask(i, parity)
                    if i < LAST:
                        bn1(i + 1, other, 0)
                        bn1(i + 1, other, 1)
                    if i >= 1:
                        bn2(i - 1, other, 0)
                    if i < LAST:
                        aggr1(i + 1, other)
                    if i >= 1:
                        bn2(i - 1, other, 1)
                    reciprocal(i, parity)
                    if i >= 1:
                        aggr2(i - 1, other)
                    if i >= 3:
                        add_bias(i - 3, other)
                        if i < LAST:
                            for h in range(NB):
                                result(i - 3, other, h)
                    if i == 0:
                        finish_weights()
                    if wide and i >= 2:
                        for h in range(NB):
                            round_wide(i - 2, parity, h)

                bn1(0, 0, 0)
                bn1(0, 0, 1)
                aggr1(0, 0)
                scale_weights()
                dve.wait_ge(tanh_made, 1)
                dve.wait_ge(consts_made, 1)
                for i in range(PAIRS):
                    step(i, i % 2)
                dve.wait_ge(rstd2_done, LAST - 1)
                dve.wait_ge(normedt_done, LAST - 1)
                residual(LAST, LAST % 2)
                bn2(LAST, LAST % 2, 0)
                variance_last(0)
                bn2(LAST, LAST % 2, 1)
                add_bias(ASIDE, ASIDE % 2)
                variance_last(1)
                for h in range(NB):
                    norm_last(h)
                    result(LAST - 3, 1 - LAST % 2, h)
                if wide:
                    for h in range(NB):
                        round_wide(LAST - 1, 1 - LAST % 2, h)
                add_bias(LAST - 1, Y_THIRD)
                for h in range(NB):
                    result(LAST - 1, Y_THIRD, h)
                for h in range(NB):
                    if wide:
                        round_wide(LAST, LAST % 2, h)
                    finish_last(h)

            nc.vector.memset(warm_sb[:, :].bitcast(F32), 0.0).then_inc(zeros_made, 1)
            centre_weights()
            centre_bias()
            scales()
            steps_before = made[0]
            branch(dve, program)

        @block.tensor
        def _(pe):
            def keys(p, s, o):
                if o == 0:
                    pe.wait_ge(ctxt_landed[s], landed_count(p, s))
                    if p == 1:
                        pe.wait_ge(first_keys_copied, 1)
                    elif p > 1:
                        pe.wait_ge(keys_copied, p - 1)
                for c in range(DC):
                    if p == 0:
                        pe.wait_ge(w_centred, o * DC + c + 1)
                    ins = nc.tensor.matmul(keys_at(p, o), wc_sb[:, c, o * P:(o + 1) * P],
                                           ctxt_sb[:, cols(p, c * NB * P, NB * P)],
                                           start=(c == 0), stop=(c == DC - 1))
                if o == DC - 1 or p == 0:
                    ins.then_inc(keys_done, 1)

            def scores_product(s, h, c):
                return nc.tensor.matmul(scores_ps[h][:, 0:P], xt_sb[:, s, c, h, :], keys_sb[:, s, c, h, :],
                                        start=(c == 0), stop=(c == DC - 1))

            def first_scores():
                pe.wait_ge(xt_landed[0], landed_count(0, 0))
                for c in range(DC):
                    pe.wait_ge(first_keys_copied, c + 1)
                    for h in range(NB):
                        ins = scores_product(0, h, c)
                        if c == DC - 1:
                            ins.then_inc(scores_done, 1)

            def scores(p, s):
                pe.wait_ge(xt_landed[s], landed_count(p, s))
                pe.wait_ge(keys_copied, p)
                pe.wait_ge(masked, p * NB)
                for h in range(NB):
                    for c in range(DC):
                        ins = scores_product(s, h, c)
                    ins.then_inc(scores_done, 1)

            def transpose_probs(p, s):
                pe.wait_ge(probs_done, p * NB + NB)
                if p != 0:
                    pe.wait_ge(probst_copied, p)
                for h in range(NB):
                    ins = nc.tensor.transpose(probst_ps[:, h, :], probs_sb[:, s, h], ident_sb[:, :])
                ins.then_inc(probst_done, 1)

            def transpose_probs_last(h):
                pe.wait_ge(probs_done, LAST * NB + h + 1)
                if h == 0:
                    pe.wait_ge(probst_copied, LAST)
                nc.tensor.transpose(probst_at(h), probs_sb[:, LAST % 2, h], ident_sb[:, :]).then_inc(probst_done, 1)

            def attend(p, s):
                pe.wait_ge(ctx_landed[s], landed_count(p, s))
                if p != 0:
                    pe.wait_ge(resid_done, p * NB)
                for h in range(NB):
                    if h == 0 or p == LAST:
                        pe.wait_ge(probst_copied, p + 1 + h)
                    nc.tensor.matmul(attn_ps[h][:, 0:D], probst_sb[:, s, h], ctx_sb[:, cols(p, h * D, D)],
                                     start=True, stop=True).then_inc(attn_done, 1)

            def transpose_normed(p, s, batches):
                pe.wait_ge(normed, p * NB + batches[-1] + 1)
                if p > 0 and batches[0] == 0:
                    pe.wait_ge(quantized, transposed_count(p - 1, 0))
                elif p == LAST - 1:
                    pe.wait_ge(probst_copied, LAST + NB)
                elif p == LAST:
                    pe.wait_ge(masked, PAIRS * NB)
                for h in batches:
                    for c in range(DC):
                        ins = nc.tensor.transpose(normedt_at(p, h)[:, c, :], normed_sb[:, s, h, c, :], identb_sb[:, :])
                ins.then_inc(normedt_done, 1)

            def ffn(p, s, batches, wide):
                pe.wait_ge(quantized, transposed_count(p, batches[-1]))
                if p == 0:
                    pe.wait_ge(wq_made, 1)
                elif p < LAST:
                    pe.wait_ge(y_copied, p)
                elif batches[0] == 0:
                    pe.wait_ge(resid_done, LAST * NB + 1)
                else:
                    pe.wait_ge(masked, PAIRS * NB)
                operand = wide_sb if wide else quant_sb
                for h in batches:
                    for c in range(DC):
                        ins = nc.tensor.matmul(ffn_at(p, h), operand[:, s, h, c, :], wq_sb[:, c, :],
                                               start=(c == 0), stop=(c == DC - 1))
                ins.then_inc(ffn_done, 1)

            def program(wide):
                def step(i, parity):
                    if i == 0:
                        first_scores()
                    else:
                        scores(i, parity)
                    if i < LAST:
                        keys(i + 1, 1 - parity, 0)
                    if i >= 2:
                        transpose_normed(i - 2, parity, range(NB))
                    if i < LAST:
                        transpose_probs(i, parity)
                        keys(i + 1, 1 - parity, 1)
                        if i >= 2:
                            ffn(i - 2, parity, range(NB), wide)
                        attend(i, parity)
                    else:
                        for h in range(NB):
                            transpose_probs_last(h)
                        attend(i, parity)
                        ffn(i - 2, parity, range(NB), wide)

                pe.wait_ge(consts_made, 1)
                for i in range(PAIRS):
                    step(i, i % 2)
                for h in range(NB):
                    transpose_normed(LAST - 1, 1 - LAST % 2, [h])
                ffn(LAST - 1, 1 - LAST % 2, range(NB), wide)
                for h in range(NB):
                    transpose_normed(LAST, LAST % 2, [h])
                for h in range(NB):
                    ffn(LAST, LAST % 2, [h], wide)

            pe.wait_ge(zeros_made, 1)
            for _ in range(WARM_UP):
                nc.tensor.matmul(attn_ps[0][:, 0:PAIR], warm_sb[:, 0:P], warm_sb[:, :], start=True, stop=True)
            for o in range(DC):
                keys(0, 0, o)
            branch(pe, program)


def kernel(x, ctx_1024, g_xattn, g_ffn, L0_xattn_W_reduce, L0_xattn_b_reduce, L0_ffn_kernel, L0_ffn_input_scale,
           L0_ffn_kernel_scale, L0_ffn_bias):
    import numpy as np
    import concourse.bacc as bacc
    from concourse.bass_utils import run_bass_kernel_spmd

    x, ctx, w, wf = (np.asarray(a) for a in (x, ctx_1024, L0_xattn_W_reduce, L0_ffn_kernel))
    B, S, D = x.shape
    chunks = D // P

    def rows(a):
        return np.ascontiguousarray(a.transpose(1, 0, 2).reshape(S, B * D))

    def features(a):
        return np.ascontiguousarray(a.reshape(B // 2, 2, S, chunks, P).transpose(4, 0, 3, 1, 2).reshape(P, B * D))

    def across(a):
        return np.broadcast_to(np.asarray(a), (P, a.shape[0]))

    arrays = {
        "x": rows(x),
        "x_t": features(x),
        "ctx": rows(ctx),
        "ctx_t": features(ctx),
        "w_t": np.ascontiguousarray(w.T.reshape(chunks, P, D).transpose(1, 0, 2).reshape(P, chunks * D)),
        "small": np.concatenate([*(across(a) for a in (g_xattn, g_ffn, L0_ffn_input_scale, L0_ffn_kernel_scale)),
                                 np.asarray(L0_xattn_b_reduce).reshape(chunks, P).T, across(L0_xattn_b_reduce)], axis=1),
        "ffn_consts": np.concatenate([wf.reshape(chunks, P, D).transpose(1, 0, 2).reshape(P, chunks * D),
                                      across(L0_ffn_bias), across(L0_ffn_bias)], axis=1),
    }
    nc = bacc.Bacc("TRN2", target_bir_lowering=False, num_devices=1)
    args = [nc.dram_tensor(f"in_{name}", a.shape, mybir.dt.from_np(a.dtype), kind="ExternalInput").ap()
            for name, a in arrays.items()]
    out = nc.dram_tensor("out", (S, B * D), F32, kind="ExternalOutput").ap()
    flamingo_block(nc, *args, out)
    r = run_bass_kernel_spmd(nc, [{f"in_{name}": a for name, a in arrays.items()}], core_ids=[0])
    got = r.results[0]["out"]
    return np.ascontiguousarray(got.reshape(S, B, D).transpose(1, 0, 2))
```
